# Optimizing a Trainium2 kernel written in Bass

```python
import numpy as np
import jax
import jax.numpy as jnp

def _softmax(x, axis=-1):
    return jax.nn.softmax(x, axis=axis)

def _gelu(x):
    return jax.nn.gelu(x, approximate=True)

def _silu(x):
    return jax.nn.silu(x)

def _sigmoid(x):
    return jax.nn.sigmoid(x)

def _layernorm(x, axis=-1, eps=1e-05):
    m = jnp.mean(x, axis=axis, keepdims=True)
    v = jnp.var(x, axis=axis, keepdims=True)
    return (x - m) / jnp.sqrt(v + eps)

def _scatter_add(tgt, idx, src, axis=0):
    return tgt.at[idx].add(src)

def _segment_sum(src, seg, n):
    return jax.ops.segment_sum(src, seg, n)
kernel_name = 'mk_dlrm_tower_d1_rec_r8_d8b130'

def setup_inputs(seed: int=0):
    np.random.seed(seed)
    _w = jnp.asarray

    def _rec_inputs():
        import jax
        import jax.numpy as jnp
        _tk = jax.random.key(seed)
        dense_ctx = jax.random.normal(jax.random.fold_in(_tk, 190), (1024, 16), jnp.float32)
        ids = jnp.stack([jax.random.randint(jax.random.fold_in(_tk, 200 + f), (1024,), 0, v, jnp.int32) for f, v in enumerate([125000, 1250, 1000, 1000, 1000, 125000, 12500, 1250, 1250, 1000, 125000, 12500, 125000, 1000, 12500, 1000, 1250, 1000, 125000, 1250, 1000, 1000, 1250, 1250])], axis=1)
        tbl_0 = 0.05 * jax.random.normal(jax.random.fold_in(_tk, 500 + 0), (125000, 16), jnp.float32)
        tbl_1 = 0.05 * jax.random.normal(jax.random.fold_in(_tk, 500 + 1), (1250, 16), jnp.float32)
        tbl_2 = 0.05 * jax.random.normal(jax.random.fold_in(_tk, 500 + 2), (1000, 16), jnp.float32)
        tbl_3 = 0.05 * jax.random.normal(jax.random.fold_in(_tk, 500 + 3), (1000, 16), jnp.float32)
        tbl_4 = 0.05 * jax.random.normal(jax.random.fold_in(_tk, 500 + 4), (1000, 16), jnp.float32)
        tbl_5 = 0.05 * jax.random.normal(jax.random.fold_in(_tk, 500 + 5), (125000, 16), jnp.float32)
        tbl_6 = 0.05 * jax.random.normal(jax.random.fold_in(_tk, 500 + 6), (12500, 16), jnp.float32)
        tbl_7 = 0.05 * jax.random.normal(jax.random.fold_in(_tk, 500 + 7), (1250, 16), jnp.float32)
        tbl_8 = 0.05 * jax.random.normal(jax.random.fold_in(_tk, 500 + 8), (1250, 16), jnp.float32)
        tbl_9 = 0.05 * jax.random.normal(jax.random.fold_in(_tk, 500 + 9), (1000, 16), jnp.float32)
        tbl_10 = 0.05 * jax.random.normal(jax.random.fold_in(_tk, 500 + 10), (125000, 16), jnp.float32)
        tbl_11 = 0.05 * jax.random.normal(jax.random.fold_in(_tk, 500 + 11), (12500, 16), jnp.float32)
        tbl_12 = 0.05 * jax.random.normal(jax.random.fold_in(_tk, 500 + 12), (125000, 16), jnp.float32)
        tbl_13 = 0.05 * jax.random.normal(jax.random.fold_in(_tk, 500 + 13), (1000, 16), jnp.float32)
        tbl_14 = 0.05 * jax.random.normal(jax.random.fold_in(_tk, 500 + 14), (12500, 16), jnp.float32)
        tbl_15 = 0.05 * jax.random.normal(jax.random.fold_in(_tk, 500 + 15), (1000, 16), jnp.float32)
        tbl_16 = 0.05 * jax.random.normal(jax.random.fold_in(_tk, 500 + 16), (1250, 16), jnp.float32)
        tbl_17 = 0.05 * jax.random.normal(jax.random.fold_in(_tk, 500 + 17), (1000, 16), jnp.float32)
        tbl_18 = 0.05 * jax.random.normal(jax.random.fold_in(_tk, 500 + 18), (125000, 16), jnp.float32)
        tbl_19 = 0.05 * jax.random.normal(jax.random.fold_in(_tk, 500 + 19), (1250, 16), jnp.float32)
        tbl_20 = 0.05 * jax.random.normal(jax.random.fold_in(_tk, 500 + 20), (1000, 16), jnp.float32)
        tbl_21 = 0.05 * jax.random.normal(jax.random.fold_in(_tk, 500 + 21), (1000, 16), jnp.float32)
        tbl_22 = 0.05 * jax.random.normal(jax.random.fold_in(_tk, 500 + 22), (1250, 16), jnp.float32)
        tbl_23 = 0.05 * jax.random.normal(jax.random.fold_in(_tk, 500 + 23), (1250, 16), jnp.float32)
        _rk = jax.random.fold_in(_tk, 7)
        W_top1 = 0.0693375 * jax.random.normal(jax.random.fold_in(_tk, 801), (208, 512), jnp.float32)
        W_top2 = 0.0441942 * jax.random.normal(jax.random.fold_in(_tk, 802), (512, 256), jnp.float32)
        W_top3 = 0.0625 * jax.random.normal(jax.random.fold_in(_tk, 803), (256, 1), jnp.float32)
        b_top1 = jnp.zeros((512,), jnp.float32)
        b_top2 = jnp.zeros((256,), jnp.float32)
        return (dense_ctx, ids, tbl_0, tbl_1, tbl_2, tbl_3, tbl_4, tbl_5, tbl_6, tbl_7, tbl_8, tbl_9, tbl_10, tbl_11, tbl_12, tbl_13, tbl_14, tbl_15, tbl_16, tbl_17, tbl_18, tbl_19, tbl_20, tbl_21, tbl_22, tbl_23, W_top1, b_top1, W_top2, b_top2, W_top3)
    dense_ctx, ids, tbl_0, tbl_1, tbl_2, tbl_3, tbl_4, tbl_5, tbl_6, tbl_7, tbl_8, tbl_9, tbl_10, tbl_11, tbl_12, tbl_13, tbl_14, tbl_15, tbl_16, tbl_17, tbl_18, tbl_19, tbl_20, tbl_21, tbl_22, tbl_23, W_top1, b_top1, W_top2, b_top2, W_top3 = _rec_inputs()

    def _L0_rec_setup():
        import jax, jax.numpy as jnp
        import numpy as np
        B, F, D = (512, 24, 16)
        LAYER_SIZES = [64, 64, 64]

        def _cin_forward(X0, Ws):
            F_ = X0.shape[1]
            Xk = X0
            outs = []
            for W in Ws:
                H_prev = Xk.shape[1]
                Wr = W.reshape(F_, H_prev, W.shape[1])
                Xk = jnp.einsum('bfd,bhd,fho->bod', X0, Xk, Wr)
                outs.append(Xk.sum(axis=2))
            return jnp.concatenate(outs, axis=1)
        key = jax.random.key(seed)
        k0, k1, k2, k3 = jax.random.split(key, 4)
        X0 = jax.random.normal(k0, (B, F, D), dtype=jnp.float32)
        prev = F
        Ws = []
        for k, h in zip((k1, k2, k3), LAYER_SIZES):
            Ws.append(jax.random.normal(k, (prev * F, h), dtype=jnp.float32) * 0.01)
            prev = h
        return {'X0': X0, 'W0': Ws[0], 'W1': Ws[1], 'W2': Ws[2]}
    _L0_rec_all = _L0_rec_setup()
    _L0_rec_in = {k: v for k, v in _L0_rec_all.items() if k in ('W0', 'W1', 'W2')}
    del _L0_rec_all
    return {'dense_ctx': dense_ctx, 'ids': ids, 'tbl_0': tbl_0, 'tbl_1': tbl_1, 'tbl_2': tbl_2, 'tbl_3': tbl_3, 'tbl_4': tbl_4, 'tbl_5': tbl_5, 'tbl_6': tbl_6, 'tbl_7': tbl_7, 'tbl_8': tbl_8, 'tbl_9': tbl_9, 'tbl_10': tbl_10, 'tbl_11': tbl_11, 'tbl_12': tbl_12, 'tbl_13': tbl_13, 'tbl_14': tbl_14, 'tbl_15': tbl_15, 'tbl_16': tbl_16, 'tbl_17': tbl_17, 'tbl_18': tbl_18, 'tbl_19': tbl_19, 'tbl_20': tbl_20, 'tbl_21': tbl_21, 'tbl_22': tbl_22, 'tbl_23': tbl_23, 'W_top1': W_top1, 'b_top1': b_top1, 'W_top2': W_top2, 'b_top2': b_top2, 'W_top3': W_top3, 'L0_rec_W0': _L0_rec_in['W0'], 'L0_rec_W1': _L0_rec_in['W1'], 'L0_rec_W2': _L0_rec_in['W2']}

def reference(dense_ctx, ids, tbl_0, tbl_1, tbl_2, tbl_3, tbl_4, tbl_5, tbl_6, tbl_7, tbl_8, tbl_9, tbl_10, tbl_11, tbl_12, tbl_13, tbl_14, tbl_15, tbl_16, tbl_17, tbl_18, tbl_19, tbl_20, tbl_21, tbl_22, tbl_23, W_top1, b_top1, W_top2, b_top2, W_top3, L0_rec_W0, L0_rec_W1, L0_rec_W2):
    import jax
    import jax.numpy as jnp

    def _L0_rec_ref(X0, W0, W1, W2):
        import jax, jax.numpy as jnp
        import numpy as np
        B, F, D = (512, 24, 16)
        LAYER_SIZES = [64, 64, 64]

        def _cin_forward(X0, Ws):
            F_ = X0.shape[1]
            Xk = X0
            outs = []
            for W in Ws:
                H_prev = Xk.shape[1]
                Wr = W.reshape(F_, H_prev, W.shape[1])
                Xk = jnp.einsum('bfd,bhd,fho->bod', X0, Xk, Wr)
                outs.append(Xk.sum(axis=2))
            return jnp.concatenate(outs, axis=1)
        return _cin_forward(X0, (W0, W1, W2))
    e = jnp.stack([tbl_0[ids[:, 0]], tbl_1[ids[:, 1]], tbl_2[ids[:, 2]], tbl_3[ids[:, 3]], tbl_4[ids[:, 4]], tbl_5[ids[:, 5]], tbl_6[ids[:, 6]], tbl_7[ids[:, 7]], tbl_8[ids[:, 8]], tbl_9[ids[:, 9]], tbl_10[ids[:, 10]], tbl_11[ids[:, 11]], tbl_12[ids[:, 12]], tbl_13[ids[:, 13]], tbl_14[ids[:, 14]], tbl_15[ids[:, 15]], tbl_16[ids[:, 16]], tbl_17[ids[:, 17]], tbl_18[ids[:, 18]], tbl_19[ids[:, 19]], tbl_20[ids[:, 20]], tbl_21[ids[:, 21]], tbl_22[ids[:, 22]], tbl_23[ids[:, 23]]], axis=1)
    z = _L0_rec_ref(e, L0_rec_W0, L0_rec_W1, L0_rec_W2)
    z = z.reshape(z.shape[0], -1)
    h = jnp.concatenate([z, dense_ctx], axis=1)
    h = jnp.maximum(h @ W_top1 + b_top1, 0.0)
    h = jnp.maximum(h @ W_top2 + b_top2, 0.0)
    y = h @ W_top3
    return y

_drawn_inputs = setup_inputs


def setup_inputs(seed=0):
    import zlib

    import numpy as np

    out = dict(_drawn_inputs(seed))
    spreads = {'b_top1': (0.0, 0.1), 'b_top2': (0.0, 0.1)}
    factors = {'tbl_0': 8.0,
     'tbl_1': 8.0,
     'tbl_2': 8.0,
     'tbl_3': 8.0,
     'tbl_4': 8.0,
     'tbl_5': 8.0,
     'tbl_6': 8.0,
     'tbl_7': 8.0,
     'tbl_8': 8.0,
     'tbl_9': 8.0,
     'tbl_10': 8.0,
     'tbl_11': 8.0,
     'tbl_12': 8.0,
     'tbl_13': 8.0,
     'tbl_14': 8.0,
     'tbl_15': 8.0,
     'tbl_16': 8.0,
     'tbl_17': 8.0,
     'tbl_18': 8.0,
     'tbl_19': 8.0,
     'tbl_20': 8.0,
     'tbl_21': 8.0,
     'tbl_22': 8.0,
     'tbl_23': 8.0,
     'L0_rec_W0': 8.0,
     'L0_rec_W1': 8.0,
     'L0_rec_W2': 8.0}
    for name, (base, spread) in spreads.items():
        noise = np.random.default_rng([zlib.crc32(name.encode()), seed]).standard_normal(out[name].shape)
        drawn = base * np.exp(spread * noise) if base else spread * noise
        out[name] = jnp.asarray(drawn.astype(out[name].dtype))
    for name, factor in factors.items():
        out[name] = (out[name] * factor).astype(out[name].dtype)
    return out
```

```python
from contextlib import ExitStack

import concourse.bass as bass
from concourse import mybir

F32 = mybir.dt.float32
ALU = mybir.AluOpType
ACT = mybir.ActivationFunctionType
AX = mybir.AxisListType

BATCH, F, D, H, DENSE = 1024, 24, 16, 64, 16
M1, M2 = 512, 256
TILE_ROWS = 128
TILES = BATCH // TILE_ROWS
UNITS = 2 * TILES
COLS = TILE_ROWS * D // 2
HALF = COLS // 2
RB = 8
KB = HALF // 128
FR, HR = 8, 16
NI, NJ = F // FR, H // HR
NP2 = NI * NJ
J3 = F // 2 + 1
ROWS_Q = KB * RB
ZR = 5

BEFORE = 3
SLOT = [("x2", n) for n in range(BEFORE)] + [("x1", i) for i in range(NI)] + \
       [("x2", n) for n in range(BEFORE, NP2)]
LAST_SLOT = [s for s in SLOT if s[0] == "x2"]
PER_SLOT = len(SLOT)
POS = {s: n for n, s in enumerate(SLOT)}
assert PER_SLOT % ZR == 0


def made(u, what):
    return NI + PER_SLOT * u + POS[what] + 1


def cin_tower(nc, dense_t, ids, tables, w0a, w0b, w1, w2, wt1, bt1, wt2, bt2, wt3, ident, mask, out):
    x0_dram = nc.dram_tensor("x0_scratch", [TILES, F + FR, 2, COLS], F32, kind="Internal").ap()
    x1_dram = nc.dram_tensor("x1_scratch", [UNITS, H, 2, HALF], F32, kind="Internal").ap()

    ctx = ExitStack()
    with ctx:
        def sb(name, shape, dt=F32):
            return ctx.enter_context(nc.sbuf_tensor(name, shape, dt))

        def bank(name):
            return ctx.enter_context(nc.psum_tensor(name, [128, 512], F32))

        def sem(name):
            return ctx.enter_context(nc.semaphore(name))

        ids_sb = sb("ids_sb", [128, TILES * F], mybir.dt.int32)
        ids_tile = sb("ids_tile", [128, F], mybir.dt.int32)
        id_sb = sb("id_sb", [128, 128])
        mask_sb = sb("mask_sb", [128, RB])
        w0_sb = sb("w0_sb", [128, NI, H])
        w0m_sb = sb("w0m_sb", [128, NI, H])
        w0s_sb = sb("w0s_sb", [128, NI, H])
        w1_sb = sb("w1_sb", [128, NP2, H])
        w2_sb = sb("w2_sb", [128, F // 2, H])
        wt1a_sb = sb("wt1a_sb", [H + DENSE, M1])
        wt1b_sb = sb("wt1b_sb", [2 * H, M1])
        wt2_sb = sb("wt2_sb", [128, M1 // 128, M2])
        wt3_sb = sb("wt3_sb", [128, M2 // 128])
        bt1_sb = sb("bt1_sb", [128, M1 // 128])
        bt2_sb = sb("bt2_sb", [128, M2 // 128])
        x0_rows = sb("x0_rows", [128, F * D])
        x0_cols = sb("x0_cols", [F, 2 * COLS])
        A = [[sb(f"A{e}{i}", [128, COLS]) for i in range(NI)] for e in range(2)]
        B = [[sb(f"B{e}{j}", [128, COLS]) for j in range(NJ)] for e in range(2)]
        C = [sb(f"C{i}", [128, COLS]) for i in range(NI)]
        Z = [sb(f"Z{r}", [128, COLS]) for r in range(ZR)]
        x0_unit = [sb(f"x0_unit{e}", [F, COLS]) for e in range(2)]
        x1_sb = sb("x1_sb", [128, HALF])
        x2_sb = sb("x2_sb", [128, HALF])
        x2_rows = sb("x2_rows", [128, KB, 128])
        x0_diag = [sb(f"x0_diag{e}", [128, 2 * KB, 2, J3, RB]) for e in range(2)]
        G = sb("G", [128, J3, BATCH])
        z1_q = sb("z1_q", [128, BATCH // 2])
        z1_dense = sb("z1_dense", [H + DENSE, BATCH])
        z23 = sb("z23", [128, BATCH])
        h1 = [[A[e][i] for e in range(2) for i in range(NI)][m] for m in range(M1 // 128)]
        h2 = [B[0][m] for m in range(M2 // 128)]
        y_sb = B[1][0][0:1, :]

        ps_x2 = [bank(f"ps_x2{e}") for e in range(2)]
        ps_x1 = bank("ps_x1")
        ps_x2r = bank("ps_x2r")
        ps_x0r = bank("ps_x0r")
        ps_g = [bank(f"ps_g{q}") for q in range(2)]
        ps_x0 = bank("ps_x0")

        ids_in = sem("ids_in")
        gathered = sem("gathered")
        ident_in, mask_in, w0_in, w1_in, tower_in = (sem(n) for n in (
            "ident_in", "mask_in", "w0_in", "w1_in", "tower_in"))
        A_in = [[sem(f"A_in{e}{i}") for i in range(NI)] for e in range(2)]
        B_in = [[sem(f"B_in{e}{j}") for j in range(NJ)] for e in range(2)]
        C_in = [sem(f"C_in{i}") for i in range(NI)]
        x0_unit_in = [sem(f"x0_unit_in{e}") for e in range(2)]
        x0_stored, x1_stored, y_stored = sem("x0_stored"), sem("x1_stored"), sem("y_stored")
        ids_ready = sem("ids_ready")
        gathers_begun, x0_turns_begun = sem("gathers_begun"), sem("x0_turns_begun")
        x0_turned = sem("x0_turned")
        z_used = sem("z_used")
        x2_turned, x0r_turned = sem("x2_turned"), sem("x0r_turned")
        g_summed = sem("g_summed")
        z3_summed, h1_summed, h2_summed, y_summed = (sem(n) for n in (
            "z3_summed", "h1_summed", "h2_summed", "y_summed"))
        x0_copied, x1_copied, x2_copied, x2r_copied = (sem(n) for n in (
            "x0_copied", "x1_copied", "x2_copied", "x2r_copied"))
        diag_ready, g_copied = sem("diag_ready"), sem("g_copied")
        z_ready2, h1_ready, h2_ready, y_ready = (sem(n) for n in (
            "z_ready2", "h1_ready", "h2_ready", "y_ready"))
        z_ready = sem("z_ready")
        z1_ready = sem("z1_ready")
        w0_ready = sem("w0_ready")
        diag_fixed = sem("diag_fixed")

        def after(engine, semaphore, count):
            if not isinstance(count, int) or count > 0:
                engine.wait_ge(semaphore, count)

        block = ctx.enter_context(nc.Block())

        @block.gpsimd
        def _(pool):
            pool.dma_start(ids_sb[:, :], ids).then_inc(ids_in, 16)
            pool.wait_ge(ids_in, 16)

            def gather(t):
                if not isinstance(t, int):
                    pool.wait_ge(x0_turned, 4 * t)
                pool.tensor_copy(ids_tile[:, :], ids_sb[:, bass.ds(t * F, F)]).then_inc(ids_ready, 1)
                pool.wait_ge(ids_ready, t + 1)
                pool.sem_inc(gathers_begun, 1)
                for f in range(F):
                    pool.indirect_dma_start(
                        out=x0_rows[:, f * D:(f + 1) * D], out_offset=None, in_=tables[f],
                        in_offset=bass.IndirectOffsetOnAxis(ap=ids_tile[:, f:f + 1], axis=0),
                    ).then_inc(gathered, 16)

            gather(0)
            with pool.Fori(1, TILES) as t:
                gather(t)

        @block.sync
        def _(sp):
            sp.dma_start(id_sb[:, :], ident).then_inc(ident_in, 16)
            sp.dma_start(w0_sb[:, :, :], w0a).then_inc(w0_in, 16)
            sp.dma_start(w0m_sb[:, :, :], w0b).then_inc(w0_in, 16)
            sp.dma_start(mask_sb[:, :], mask).then_inc(mask_in, 16)
            sp.dma_start(w1_sb[:, :, :], w1).then_inc(w1_in, 16)

            def load_a(t, e, i):
                src = x0_dram[bass.ds(t, 1), FR * i:FR * (i + 1), e, :].rearrange("t f c -> (t f) c")
                sp.dma_start(A[e][i][:, :], src.unsqueeze(1).to_broadcast([FR, HR, COLS]))\
                    .then_inc(A_in[e][i], 16)

            def load_c(t, e, i):
                src = x0_dram[bass.ds(t, 1), FR * i:FR * i + HR, e, :].rearrange("t f c -> t (f) c")
                sp.dma_start(C[i][:, :], src.to_broadcast([FR, HR, COLS])).then_inc(C_in[i], 16)

            def load_b(u, e, j):
                src = x1_dram[bass.ds(u, 1), HR * j:HR * (j + 1), :, :].rearrange("u h q c -> u h (q c)")
                sp.dma_start(B[e][j][:, :], src.to_broadcast([FR, HR, COLS])).then_inc(B_in[e][j], 16)

            def load_x0_unit(t, e):
                src = x0_dram[bass.ds(t, 1), 0:F, e, :].rearrange("t f c -> (t f) c")
                sp.dma_start(x0_unit[e][:, :], src).then_inc(x0_unit_in[e], 16)

            sp.wait_ge(x0_stored, 32)
            for i in range(NI):
                load_a(0, 0, i)
                load_c(0, 0, i)
            for i in range(NI):
                load_a(0, 1, i)
            load_x0_unit(0, 0)
            load_x0_unit(0, 1)
            sp.wait_ge(x1_stored, 16)
            for j in range(NJ):
                load_b(0, 0, j)
            for i in range(NI):
                sp.wait_ge(z_ready, i + 1)
                load_c(0, 1, i)
            for dst, src in ((w2_sb[:, :, :], w2), (wt1a_sb[:, :], wt1[0]), (wt1b_sb[:, :], wt1[1]),
                             (wt2_sb[:, :, :], wt2), (wt3_sb[:, :], wt3), (bt1_sb[:, :], bt1),
                             (bt2_sb[:, :], bt2), (z1_dense[H:H + DENSE, :], dense_t)):
                sp.dma_start(dst, src).then_inc(tower_in, 16)
            with sp.Fori(1, TILES) as t:
                sp.wait_ge(x0_stored, 32 * (t + 1))
                for e in range(2):
                    u = 2 * t + e
                    sp.wait_ge(z_ready, made(u - 2, ("x2", NJ - 1)))
                    load_a(t, e, 0)
                    for i in range(NI):
                        sp.wait_ge(z_ready, made(u - 2, ("x1", i)))
                        load_c(t, e, i)
                    sp.wait_ge(x0r_turned, u - 1)
                    load_x0_unit(t, e)
                    sp.wait_ge(z_ready, made(u - 2, ("x2", 2 * NJ - 1)))
                    load_a(t, e, 1)
                    sp.wait_ge(x1_stored, 16 * u)
                    for j in range(NJ):
                        load_b(u - 1, 1 - e, j)
                    sp.wait_ge(z_ready, made(u - 2, ("x2", 3 * NJ - 1)))
                    load_a(t, e, 2)
            sp.wait_ge(x1_stored, 16 * UNITS)
            for j in range(NJ):
                load_b(UNITS - 1, 1, j)
            sp.wait_ge(y_ready, 2)
            sp.dma_start(out, y_sb).then_inc(y_stored, 16)
            sp.wait_ge(y_stored, 16)

        @block.vector
        def _(dve):
            dve.wait_ge(mask_in, 16)
            for e in range(2):
                for k in range(2 * KB):
                    nc.vector.tensor_copy(x0_diag[e][:, k, 0, J3 - 1, :], mask_sb[:, :])
                last = nc.vector.memset(x0_diag[e][:, :, 1, J3 - 1, :], 0.0)
            last.then_inc(diag_fixed, 1)
            dve.wait_ge(w0_in, 32)
            nc.vector.tensor_tensor(w0s_sb[:, :, :], w0_sb[:, :, :], w0m_sb[:, :, :], ALU.add)\
                .then_inc(w0_ready, 1)

            def product(s):
                after(dve, z_used, s - ZR + 1)

            def cross1(u, t, e, i, s, r):
                dve.wait_ge(A_in[e][i], 16 * (t + 1))
                dve.wait_ge(C_in[i], 16 * (u + 1))
                product(s)
                nc.vector.tensor_tensor(Z[r][:, :], A[e][i][:, :], C[i][:, :], ALU.mult)\
                    .then_inc(z_ready, 1)

            def cross2(t, e, n, s, r):
                i, j = n // NJ, n % NJ
                if i == 0:
                    dve.wait_ge(B_in[e][j], 16 * (t + 1))
                product(s)
                nc.vector.tensor_tensor(Z[r][:, :], A[e][i][:, :], B[e][j][:, :], ALU.mult)\
                    .then_inc(z_ready, 1)

            def sum_x1(u):
                dve.wait_ge(x1_copied, u + 1)
                nc.vector.tensor_reduce(
                    z1_q[:, bass.ds(u * ROWS_Q, ROWS_Q)].rearrange("p (k b) -> p k b", b=RB),
                    x1_sb[:, :].rearrange("p (k d b) -> p k b d", d=D, b=RB), AX.X, ALU.add)\
                    .then_inc(z1_ready, 1)

            def slot(t, e, order):
                u = 2 * t + e
                for pos, (kind, n) in enumerate(order):
                    s = NI + PER_SLOT * u + pos
                    r = (NI + pos) % ZR
                    if kind == "x1":
                        cross1(u + 1, t + e, 1 - e, n, s, r)
                    else:
                        cross2(t, e, n, s, r)
                    if pos == 10 and order is SLOT:
                        sum_x1(u + 1)

            for i in range(NI):
                cross1(0, 0, 0, i, i, i)
            sum_x1(0)
            slot(0, 0, SLOT)
            slot(0, 1, SLOT)
            with dve.Fori(1, TILES - 1) as t:
                slot(t, 0, SLOT)
                slot(t, 1, SLOT)
            slot(TILES - 1, 0, SLOT)
            slot(TILES - 1, 1, LAST_SLOT)

        def mm(out, lhsT, rhs, start=True, stop=True):
            return nc.tensor.matmul(out, lhsT, rhs, start=start, stop=stop)

        @block.tensor
        def _(pe):
            def turn_x0(t, g):
                if g == 0:
                    pe.wait_ge(gathered, 16 * F * (t + 1))
                after(pe, x0_copied, 4 * t + g)
                for d in range(4):
                    last = nc.tensor.transpose(ps_x0[0:F, 128 * d:128 * (d + 1)],
                                               x0_rows[:, 4 * g + d:F * D:D], id_sb[:, :])
                last.then_inc(x0_turned, 1)

            def cross1(u, i, s, r):
                if i == 0:
                    after(pe, x1_copied, u)
                pe.wait_ge(z_ready, s + 1)
                for q in range(2):
                    m = mm(ps_x1[H * q:H * (q + 1), :], w0s_sb[:, i, :], Z[r][:, HALF * q:HALF * (q + 1)],
                           i == 0, i == NI - 1)
                m.then_inc(z_used, 1)

            def cross2(u, e, n, s, r):
                if n == 0:
                    after(pe, x2_copied, u - 1)
                pe.wait_ge(z_ready, s + 1)
                for q in range(2):
                    m = mm(ps_x2[e][H * q:H * (q + 1), :], w1_sb[:, n, :], Z[r][:, HALF * q:HALF * (q + 1)],
                           n == 0, n == NP2 - 1)
                m.then_inc(z_used, 1)

            def turn_x2(u):
                pe.wait_ge(x2_copied, u + 1)
                after(pe, x2r_copied, u)
                for k in range(KB):
                    last = nc.tensor.transpose(ps_x2r[:, 128 * k:128 * (k + 1)],
                                               x2_sb[:, 128 * k:128 * (k + 1)], id_sb[:, :])
                last.then_inc(x2_turned, 1)

            def turn_x0_unit(u, t, e):
                pe.wait_ge(x0_unit_in[e], 16 * (t + 1))
                after(pe, diag_ready, u)
                pe.sem_inc(x0_turns_begun, 1)
                for k in range(2 * KB):
                    last = nc.tensor.transpose(ps_x0r[:, F * k:F * (k + 1)],
                                               x0_unit[e][:, 128 * k:128 * (k + 1)], id_sb[0:F, 0:F])
                last.then_inc(x0r_turned, 1)

            def sum_g(u, e, q):
                if q == 0:
                    pe.wait_ge(x2r_copied, u + 1)
                    pe.wait_ge(diag_ready, u + 1)
                if not (isinstance(u, int) and u < 1):
                    pe.wait_ge(g_copied, 2 * u - 1 + q)
                for k in range(KB):
                    for par in range(2):
                        last = mm(ps_g[q][H * par:H * (par + 1), J3 * RB * k:J3 * RB * (k + 1)],
                                  x2_rows[:, k, H * q:H * (q + 1)],
                                  x0_diag[e][:, KB * q + k, par, :, :].rearrange("p j b -> p (j b)"))
                last.then_inc(g_summed, 1)

            def slot(t, e, order, back=True, front=True):
                u = 2 * t + e
                for pos, (kind, n) in enumerate(order):
                    s = NI + PER_SLOT * u + pos
                    r = (NI + pos) % ZR
                    if kind == "x1":
                        cross1(u + 1, n, s, r)
                        continue
                    cross2(u, e, n, s, r)
                    if e == 0 and front and n < 4:
                        turn_x0(t + 1, n)
                    if back and n == 1:
                        turn_x2(u - 1)
                    if back and n in (3, 4):
                        sum_g(u - 1, 1 - e, n - 3)
                    if n == 7:
                        turn_x0_unit(u, t, e)

            pe.wait_ge(ident_in, 16)
            for g in range(4):
                turn_x0(0, g)
            pe.wait_ge(w0_ready, 1)
            for i in range(NI):
                cross1(0, i, i, i)
            pe.wait_ge(w1_in, 16)
            slot(0, 0, SLOT, back=False)
            pe.wait_ge(diag_fixed, 1)
            slot(0, 1, SLOT)
            with pe.Fori(1, TILES - 1) as t:
                slot(t, 0, SLOT)
                slot(t, 1, SLOT)
            slot(TILES - 1, 0, SLOT, front=False)
            slot(TILES - 1, 1, LAST_SLOT)
            turn_x2(UNITS - 1)
            for q in range(2):
                sum_g(UNITS - 1, 1, q)

            pe.wait_ge(tower_in, 16 * 8)
            pe.wait_ge(g_copied, 2 * UNITS)
            for j in range(F // 2):
                for half in range(2):
                    last = mm(ps_x1[H * (1 - half):H * (2 - half), :], w2_sb[:, j, :],
                              G[:, j, 512 * half:512 * (half + 1)], j == 0, j == F // 2 - 1)
            last.then_inc(z3_summed, 1)
            pe.wait_ge(z_ready2, 5)
            n = 0
            for half in range(2):
                cols = slice(512 * half, 512 * (half + 1))
                for m in range(M1 // 128):
                    if n >= 2:
                        pe.wait_ge(h1_ready, n - 1)
                    ps = ps_x2[n % 2]
                    mm(ps[:, :], wt1a_sb[:, 128 * m:128 * (m + 1)], z1_dense[:, cols], True, False)
                    mm(ps[:, :], wt1b_sb[:, 128 * m:128 * (m + 1)], z23[:, cols], False, True)\
                        .then_inc(h1_summed, 1)
                    n += 1
            n = 0
            for half in range(2):
                cols = slice(512 * half, 512 * (half + 1))
                pe.wait_ge(h1_ready, (half + 1) * (M1 // 128))
                for m in range(M2 // 128):
                    if n >= 2:
                        pe.wait_ge(h2_ready, n - 1)
                    for k in range(M1 // 128):
                        last = mm(ps_g[n % 2][:, :], wt2_sb[:, k, 128 * m:128 * (m + 1)], h1[k][:, cols],
                                  k == 0, k == M1 // 128 - 1)
                    last.then_inc(h2_summed, 1)
                    n += 1
            for half in range(2):
                cols = slice(512 * half, 512 * (half + 1))
                pe.wait_ge(h2_ready, 2 * (half + 1))
                ps = (ps_x2r, ps_x0r)[half]
                for k in range(M2 // 128):
                    last = mm(ps[0:1, :], wt3_sb[:, k:k + 1], h2[k][:, cols], k == 0, k == M2 // 128 - 1)
                last.then_inc(y_summed, 1)

        @block.scalar
        def _(act):
            def copy_x0(t, g):
                if g == 0:
                    after(act, x0_stored, 32 * t)
                act.wait_ge(x0_turned, 4 * t + g + 1)
                nc.scalar.copy(
                    x0_cols[:, :].rearrange("f (k d b) -> f d k b", d=D, b=RB)[:, 4 * g:4 * (g + 1), :, :],
                    ps_x0[0:F, :].rearrange("f (d k b) -> f d k b", d=4, b=RB)).then_inc(x0_copied, 1)

            def store_x0(t):
                act.wait_ge(x0_copied, 4 * (t + 1))
                v = x0_dram[bass.ds(t, 1), :, :, :].rearrange("t f e c -> (t f) (e c)")
                act.dma_start(v[0:F, :], x0_cols[:, :]).then_inc(x0_stored, 16)
                act.dma_start(v[F:F + FR, :], x0_cols[0:FR, :]).then_inc(x0_stored, 16)

            def copy_x1(u):
                act.wait_ge(z_used, NI if isinstance(u, int) and u == 0 else made(u - 1, ("x1", NI - 1)))
                after(act, x1_stored, 16 * u)
                after(act, z1_ready, u)
                nc.scalar.copy(x1_sb[:, :], ps_x1[:, :]).then_inc(x1_copied, 1)
                act.wait_ge(x1_copied, u + 1)
                v = x1_dram[bass.ds(u, 1), :, :, :].rearrange("u h q c -> (u q) h c")
                act.dma_start(v, x1_sb[:, :]).then_inc(x1_stored, 16)

            def copy_x2(u, e, products):
                act.wait_ge(z_used, products)
                after(act, x2_turned, u)
                nc.scalar.copy(x2_sb[:, :], ps_x2[e][:, :]).then_inc(x2_copied, 1)

            def copy_x2_rows(u):
                act.wait_ge(x2_turned, u + 1)
                after(act, g_summed, 2 * u)
                nc.scalar.copy(x2_rows[:, :, :].rearrange("p k n -> p (k n)"), ps_x2r[:, :])\
                    .then_inc(x2r_copied, 1)

            def spread_x0(u, e):
                act.wait_ge(x0r_turned, u + 1)
                after(act, g_summed, 2 * (u - 1))
                for b in range(RB):
                    last = nc.scalar.activation(
                        x0_diag[e][:, :, :, 0:F // 2, b].rearrange("p k a j -> p k j a"),
                        ps_x0r[:, 0:2 * KB * F].rearrange("p (k j a) -> p k j a", k=2 * KB, a=2),
                        ACT.Copy, scale=mask_sb[:, b:b + 1])
                last.then_inc(diag_ready, 1)

            def copy_g(u, q):
                act.wait_ge(g_summed, 2 * u + q + 1)
                nc.scalar.copy(
                    G[:, :, bass.ds(q * (BATCH // 2) + u * ROWS_Q, ROWS_Q)].rearrange("p j (k b) -> p k j b", b=RB),
                    ps_g[q][:, 0:KB * J3 * RB].rearrange("p (k j b) -> p k j b", k=KB, j=J3))\
                    .then_inc(g_copied, 1)

            def slot(t, e, back=True, front=True, last=False):
                u = 2 * t + e
                if back:
                    copy_x2(u - 1, 1 - e, made(u - 1, ("x2", NP2 - 1)))
                if e == 0 and front:
                    copy_x0(t + 1, 0)
                    copy_x0(t + 1, 1)
                if back:
                    copy_x2_rows(u - 1)
                if e == 0 and front:
                    copy_x0(t + 1, 2)
                if not last:
                    copy_x1(u + 1)
                if e == 0 and front:
                    copy_x0(t + 1, 3)
                    store_x0(t + 1)
                if back:
                    copy_g(u - 1, 0)
                    copy_g(u - 1, 1)
                spread_x0(u, e)

            for g in range(4):
                copy_x0(0, g)
            store_x0(0)
            copy_x1(0)
            act.wait_ge(mask_in, 16)
            slot(0, 0, back=False)
            slot(0, 1)
            with act.Fori(1, TILES - 1) as t:
                slot(t, 0)
                slot(t, 1)
            slot(TILES - 1, 0, front=False)
            slot(TILES - 1, 1, last=True)
            copy_x2(UNITS - 1, 1, NI + PER_SLOT * UNITS - NI)
            copy_x2_rows(UNITS - 1)
            copy_g(UNITS - 1, 0)
            copy_g(UNITS - 1, 1)

            act.wait_ge(z1_ready, UNITS)
            act.wait_ge(tower_in, 16 * 8)
            act.wait_ge(g_copied, 2 * UNITS)
            for q in range(2):
                nc.scalar.copy(z1_dense[0:H, 512 * q:512 * (q + 1)], z1_q[H * q:H * (q + 1), :])\
                    .then_inc(z_ready2, 1)
            nc.scalar.copy(z23[0:H, :], G[0:H, J3 - 1, :]).then_inc(z_ready2, 1)
            act.wait_ge(z3_summed, 1)
            for half in range(2):
                nc.scalar.copy(z23[H:2 * H, 512 * half:512 * (half + 1)],
                               ps_x1[H * (1 - half):H * (2 - half), :]).then_inc(z_ready2, 1)
            n = 0
            for half in range(2):
                for m in range(M1 // 128):
                    act.wait_ge(h1_summed, n + 1)
                    nc.scalar.activation(h1[m][:, 512 * half:512 * (half + 1)], ps_x2[n % 2][:, :], ACT.Relu,
                                         bias=bt1_sb[:, m:m + 1]).then_inc(h1_ready, 1)
                    n += 1
            n = 0
            for half in range(2):
                for m in range(M2 // 128):
                    act.wait_ge(h2_summed, n + 1)
                    nc.scalar.activation(h2[m][:, 512 * half:512 * (half + 1)], ps_g[n % 2][:, :], ACT.Relu,
                                         bias=bt2_sb[:, m:m + 1]).then_inc(h2_ready, 1)
                    n += 1
            for half in range(2):
                act.wait_ge(y_summed, half + 1)
                nc.scalar.copy(y_sb[:, 512 * half:512 * (half + 1)], (ps_x2r, ps_x0r)[half][0:1, :])\
                    .then_inc(y_ready, 1)


def kernel(**inputs):
    import numpy as np
    import concourse.bacc as bacc
    from concourse import mybir as mb
    from concourse.bass_utils import run_bass_kernel_spmd

    a = {k: np.asarray(v) for k, v in inputs.items()}
    w0 = a["L0_rec_W0"].reshape(F, F, H)
    w0a = np.zeros((FR, HR, NI, H), w0.dtype)
    w0b = np.zeros((FR, HR, NI, H), w0.dtype)
    for i in range(NI):
        for g in range(HR):
            w0a[:, g, i] = w0[FR * i:FR * (i + 1), (FR * i + g) % F]
            if g >= FR:
                w0b[:, g, i] = w0[(FR * i + g) % F, FR * i:FR * (i + 1)]
    w1 = a["L0_rec_W1"].reshape(NI, FR, NJ, HR, H).transpose(1, 3, 0, 2, 4)
    w2 = a["L0_rec_W2"].reshape(F // 2, 128, H).transpose(1, 0, 2)
    wt1 = a["W_top1"]
    arrays = {
        "dense_t": a["dense_ctx"].reshape(TILES, 2, 2, ROWS_Q, DENSE).transpose(4, 2, 0, 1, 3).reshape(DENSE, BATCH),
        "ids": a["ids"].reshape(TILES, 128, F).transpose(1, 0, 2).reshape(128, TILES * F),
        "w0a": w0a.reshape(128, NI, H),
        "w0b": w0b.reshape(128, NI, H),
        "w1": w1.reshape(128, NP2, H),
        "w2": w2,
        "wt1_z1_dense": np.concatenate([wt1[0:H], wt1[3 * H:]], axis=0),
        "wt1_z2_z3": wt1[H:3 * H],
        "bt1": a["b_top1"].reshape(M1 // 128, 128).transpose(1, 0),
        "wt2": a["W_top2"].reshape(M1 // 128, 128, M2).transpose(1, 0, 2),
        "bt2": a["b_top2"].reshape(M2 // 128, 128).transpose(1, 0),
        "wt3": a["W_top3"].reshape(M2 // 128, 128).transpose(1, 0),
        "ident": np.eye(128, dtype=np.float32),
        "mask": np.tile(np.eye(RB, dtype=np.float32), (128 // RB, 1)),
    }
    for f in range(F):
        arrays[f"tbl_{f}"] = a[f"tbl_{f}"]
    nc = bacc.Bacc("TRN2", target_bir_lowering=False, num_devices=1)
    arrays = {k: np.ascontiguousarray(v) for k, v in arrays.items()}
    ap = {k: nc.dram_tensor(k, v.shape, mb.dt.from_np(v.dtype), kind="ExternalInput").ap()
          for k, v in arrays.items()}
    out = nc.dram_tensor("y", (1, BATCH), F32, kind="ExternalOutput").ap()
    cin_tower(nc, ap["dense_t"], ap["ids"], [ap[f"tbl_{f}"] for f in range(F)], ap["w0a"], ap["w0b"],
              ap["w1"], ap["w2"], (ap["wt1_z1_dense"], ap["wt1_z2_z3"]), ap["bt1"], ap["wt2"], ap["bt2"],
              ap["wt3"], ap["ident"], ap["mask"], out)
    y = run_bass_kernel_spmd(nc, [arrays], core_ids=[0]).results[0]["y"]
    return y.reshape(2, TILES, 2, ROWS_Q).transpose(1, 2, 0, 3).reshape(BATCH, 1)
```

```python
from contextlib import ExitStack

import concourse.bass as bass
from concourse import mybir

F32 = mybir.dt.float32
ALU = mybir.AluOpType
ACT = mybir.ActivationFunctionType
AX = mybir.AxisListType

BATCH, F, D, H, DENSE = 1024, 24, 16, 64, 16
M1, M2 = 512, 256
TILE_ROWS = 128
TILES = BATCH // TILE_ROWS
UNITS = 2 * TILES
COLS = TILE_ROWS * D // 2
HALF = COLS // 2
RB = 8
KB = HALF // 128
FR, HR = 8, 16
NI, NJ = F // FR, H // HR
NP2 = NI * NJ
J3 = F // 2 + 1
ROWS_Q = KB * RB
NHALF = 2
LOADED = [slice(0, 64), slice(64, 128), slice(0, 128)]
ZR = 5

BEFORE = 2
SLOT = [("x2", n) for n in range(BEFORE)] + [("x1", i) for i in range(NI)] + \
       [("x2", n) for n in range(BEFORE, NP2)]
LAST_SLOT = [s for s in SLOT if s[0] == "x2"]
X0_STORES = 16 * (NI + 1)
PER_SLOT = len(SLOT)
POS = {s: n for n, s in enumerate(SLOT)}
assert PER_SLOT % ZR == 0


def made(u, what):
    return NI + PER_SLOT * u + POS[what] + 1


def cin_tower(nc, dense_t, ids, tables, w0a, w0b, w1, w2, wt1, bt1, wt2, bt2, wt3, ident, mask, out):
    x0_dram = nc.dram_tensor("x0_scratch", [TILES, 2, F + FR, COLS], F32, kind="Internal").ap()

    ctx = ExitStack()
    with ctx:
        def sb(name, shape, dt=F32):
            return ctx.enter_context(nc.sbuf_tensor(name, shape, dt))

        def bank(name):
            return ctx.enter_context(nc.psum_tensor(name, [128, 512], F32))

        def sem(name):
            return ctx.enter_context(nc.semaphore(name))

        ids_sb = sb("ids_sb", [128, TILES * F], mybir.dt.int32)
        ids_tile = sb("ids_tile", [128, F], mybir.dt.int32)
        id_sb = sb("id_sb", [128, 128])
        mask_sb = sb("mask_sb", [128, RB])
        w0_sb = sb("w0_sb", [128, NI, H])
        w0m_sb = sb("w0m_sb", [128, NI, H])
        w0s_sb = sb("w0s_sb", [128, NI, H])
        w1_sb = sb("w1_sb", [128, NP2, H])
        w2_sb = sb("w2_sb", [128, F // 2, H])
        wt1a_sb = sb("wt1a_sb", [H + DENSE, M1])
        wt1b_sb = sb("wt1b_sb", [2 * H, M1])
        wt2_sb = sb("wt2_sb", [128, M1 // 128, M2])
        wt3_sb = sb("wt3_sb", [128, M2 // 128])
        bt1_sb = sb("bt1_sb", [128, M1 // 128])
        bt2_sb = sb("bt2_sb", [128, M2 // 128])
        x0_rows = sb("x0_rows", [128, F * D])
        x0_cols = sb("x0_cols", [128, NI, TILE_ROWS])
        x0_blocks = sb("x0_blocks", [F, COLS])
        A = [[sb(f"A{e}{i}", [128, COLS]) for i in range(NI)] for e in range(2)]
        B = [[sb(f"B{e}{j}", [128, COLS]) for j in range(NJ)] for e in range(2)]
        C = [sb(f"C{i}", [128, COLS]) for i in range(NI)]
        Z = [sb(f"Z{r}", [128, COLS]) for r in range(ZR)]
        x0_unit = [sb(f"x0_unit{e}", [F, COLS]) for e in range(2)]
        x1_sb = sb("x1_sb", [128, HALF])
        x2_sb = sb("x2_sb", [128, HALF])
        x2_rows = sb("x2_rows", [128, KB, 128])
        x0_diag = [sb(f"x0_diag{e}", [128, 2 * KB, 2, J3, RB]) for e in range(2)]
        G = sb("G", [128, J3, BATCH])
        z1_q = sb("z1_q", [128, BATCH // 2])
        z1_dense = sb("z1_dense", [H + DENSE, BATCH])
        z23 = sb("z23", [128, BATCH])
        h1 = [[A[e][i] for e in range(2) for i in range(NI)][m] for m in range(M1 // 128)]
        h2 = [B[0][m] for m in range(M2 // 128)]
        y_sb = B[1][0][0:1, :]

        ps_x2 = [bank(f"ps_x2{e}") for e in range(2)]
        ps_x1 = bank("ps_x1")
        ps_x2r = bank("ps_x2r")
        ps_x0r = bank("ps_x0r")
        ps_g = [bank(f"ps_g{q}") for q in range(2)]
        ps_x0 = bank("ps_x0")

        ids_in = sem("ids_in")
        gathered = sem("gathered")
        ident_in, mask_in, w0_in, w1_in, tower_in = (sem(n) for n in (
            "ident_in", "mask_in", "w0_in", "w1_in", "tower_in"))
        A_in = [[sem(f"A_in{e}{i}") for i in range(NI)] for e in range(2)]
        B_in = [[sem(f"B_in{e}{j}") for j in range(NJ)] for e in range(2)]
        C_in = [sem(f"C_in{i}") for i in range(NI)]
        x0_unit_in = [sem(f"x0_unit_in{e}") for e in range(2)]
        x0_stored, y_stored = sem("x0_stored"), sem("y_stored")
        ids_ready = sem("ids_ready")
        gathers_begun, x0_turns_begun = sem("gathers_begun"), sem("x0_turns_begun")
        x0_turned = sem("x0_turned")
        z_used = sem("z_used")
        x2_turned, x0r_turned = sem("x2_turned"), sem("x0r_turned")
        g_summed = sem("g_summed")
        z3_summed, h1_summed, h2_summed, y_summed = (sem(n) for n in (
            "z3_summed", "h1_summed", "h2_summed", "y_summed"))
        x0_copied, x1_copied, x2_copied, x2r_copied = (sem(n) for n in (
            "x0_copied", "x1_copied", "x2_copied", "x2r_copied"))
        blocks_ready, diag_ready, g_copied = sem("blocks_ready"), sem("diag_ready"), sem("g_copied")
        A_ready = sem("A_ready")
        z_ready2, h1_ready, h2_ready, y_ready = (sem(n) for n in (
            "z_ready2", "h1_ready", "h2_ready", "y_ready"))
        z_ready = sem("z_ready")
        z1_ready = sem("z1_ready")
        w0_ready = sem("w0_ready")
        diag_fixed = sem("diag_fixed")

        def after(engine, semaphore, count):
            if not isinstance(count, int) or count > 0:
                engine.wait_ge(semaphore, count)

        block = ctx.enter_context(nc.Block())

        @block.gpsimd
        def _(pool):
            pool.dma_start(ids_sb[:, :], ids).then_inc(ids_in, 16)
            pool.wait_ge(ids_in, 16)

            def gather(t):
                if not isinstance(t, int):
                    pool.wait_ge(x0_turned, t)
                pool.tensor_copy(ids_tile[:, :], ids_sb[:, bass.ds(t * F, F)]).then_inc(ids_ready, 1)
                pool.wait_ge(ids_ready, t + 1)
                pool.sem_inc(gathers_begun, 1)
                for f in range(F):
                    pool.indirect_dma_start(
                        out=x0_rows[:, f * D:(f + 1) * D], out_offset=None, in_=tables[f],
                        in_offset=bass.IndirectOffsetOnAxis(ap=ids_tile[:, f:f + 1], axis=0),
                    ).then_inc(gathered, 16)

            gather(0)
            with pool.Fori(1, TILES) as t:
                gather(t)

        @block.sync
        def _(sp):
            sp.dma_start(id_sb[:, :], ident).then_inc(ident_in, 16)
            sp.dma_start(w0_sb[:, :, :], w0a).then_inc(w0_in, 16)
            sp.dma_start(w0m_sb[:, :, :], w0b).then_inc(w0_in, 16)
            sp.dma_start(mask_sb[:, :], mask).then_inc(mask_in, 16)
            sp.dma_start(w1_sb[:, :, :], w1).then_inc(w1_in, 16)

            def load_a(t, e, i):
                src = x0_dram[bass.ds(t, 1), e, FR * i:FR * (i + 1), :]
                p = LOADED[i]
                sp.dma_start(A[e][i][p, :], src.to_broadcast([(p.stop - p.start) // FR, FR, COLS]))\
                    .then_inc(A_in[e][i], 16)

            def load_c(t, e, i):
                src = x0_dram[bass.ds(t, 1), e, FR * i:FR * i + HR, :].rearrange("t f c -> (t f) c")
                sp.dma_start(C[i][:, :], src.unsqueeze(1).to_broadcast([HR, FR, COLS])).then_inc(C_in[i], 16)

            def load_b(u, e):
                sp.wait_ge(x1_copied, u + 1)
                for j in range(NJ):
                    for q in range(2):
                        src = x1_sb[H * q + HR * j:H * q + HR * (j + 1), :].unsqueeze(1)
                        sp.dma_start(B[e][j][:, HALF * q:HALF * (q + 1)], src.to_broadcast([HR, FR, HALF]))\
                            .then_inc(B_in[e][j], 16)

            def load_x0_unit(t, e):
                src = x0_dram[bass.ds(t, 1), e, 0:F, :].rearrange("t f c -> (t f) c")
                sp.dma_start(x0_unit[e][:, :], src).then_inc(x0_unit_in[e], 16)

            sp.wait_ge(x0_stored, X0_STORES)
            for i in range(NI):
                load_a(0, 0, i)
                load_c(0, 0, i)
            for i in range(NI):
                load_a(0, 1, i)
            load_x0_unit(0, 0)
            load_x0_unit(0, 1)
            load_b(0, 0)
            for i in range(NI):
                sp.wait_ge(z_ready, i + 1)
                load_c(0, 1, i)
            for dst, src in ((w2_sb[:, :, :], w2), (wt1a_sb[:, :], wt1[0]), (wt1b_sb[:, :], wt1[1]),
                             (wt2_sb[:, :, :], wt2), (wt3_sb[:, :], wt3), (bt1_sb[:, :], bt1),
                             (bt2_sb[:, :], bt2), (z1_dense[H:H + DENSE, :], dense_t)):
                sp.dma_start(dst, src).then_inc(tower_in, 16)
            with sp.Fori(1, TILES) as t:
                for e in range(2):
                    u = 2 * t + e
                    if e == 0:
                        sp.wait_ge(x0_stored, X0_STORES * (t + 1))
                    for i in range(NI):
                        sp.wait_ge(z_ready, made(u - 2, ("x1", i)))
                        load_c(t, e, i)
                    load_b(u - 1, 1 - e)
                    sp.wait_ge(z_ready, made(u - 2, ("x2", NJ - 1)))
                    load_a(t, e, 0)
                    sp.wait_ge(blocks_ready, u - 1)
                    load_x0_unit(t, e)
                    sp.wait_ge(z_ready, made(u - 2, ("x2", 2 * NJ - 1)))
                    load_a(t, e, 1)
                    sp.wait_ge(z_ready, made(u - 2, ("x2", 3 * NJ - 1)))
                    load_a(t, e, 2)
            load_b(UNITS - 1, 1)
            sp.wait_ge(y_ready, 2)
            sp.dma_start(out, y_sb).then_inc(y_stored, 16)
            sp.wait_ge(y_stored, 16)

        @block.vector
        def _(dve):
            dve.wait_ge(mask_in, 16)
            for e in range(2):
                for k in range(2 * KB):
                    nc.vector.tensor_copy(x0_diag[e][:, k, 0, J3 - 1, :], mask_sb[:, :])
                last = nc.vector.memset(x0_diag[e][:, :, 1, J3 - 1, :], 0.0)
            last.then_inc(diag_fixed, 1)
            dve.wait_ge(w0_in, 32)
            nc.vector.tensor_tensor(w0s_sb[:, :, :], w0_sb[:, :, :], w0m_sb[:, :, :], ALU.add)\
                .then_inc(w0_ready, 1)

            def by_d(x):
                return x[:, :].rearrange("p (d q b) -> p q d b", d=D, q=2)

            def by_q(x):
                return x[:, :].rearrange("p (q d b) -> p q d b", d=D, q=2)

            def product(s):
                after(dve, z_used, s - ZR + 1)

            def cross1(u, t, e, i, s, r):
                if i < NHALF:
                    dve.wait_ge(A_ready, NHALF * u + i + 1)
                else:
                    dve.wait_ge(A_in[e][i], 16 * (t + 1))
                dve.wait_ge(C_in[i], 16 * (u + 1))
                product(s)
                nc.vector.tensor_tensor(by_q(Z[r]), by_d(A[e][i]), by_d(C[i]), ALU.mult)\
                    .then_inc(z_ready, 1)

            def cross2(t, e, n, s, r):
                i, j = n // NJ, n % NJ
                if i == 0:
                    dve.wait_ge(B_in[e][j], 32 * (t + 1))
                product(s)
                nc.vector.tensor_tensor(by_q(Z[r]), by_d(A[e][i]), by_q(B[e][j]), ALU.mult)\
                    .then_inc(z_ready, 1)

            def sum_x1(u):
                dve.wait_ge(x1_copied, u + 1)
                nc.vector.tensor_reduce(
                    z1_q[:, bass.ds(u * ROWS_Q, ROWS_Q)],
                    x1_sb[:, :].rearrange("p (d b) -> p b d", d=D), AX.X, ALU.add)\
                    .then_inc(z1_ready, 1)

            def slot(t, e, order):
                u = 2 * t + e
                for pos, (kind, n) in enumerate(order):
                    s = NI + PER_SLOT * u + pos
                    r = (NI + pos) % ZR
                    if kind == "x1":
                        cross1(u + 1, t + e, 1 - e, n, s, r)
                    else:
                        cross2(t, e, n, s, r)
                    if pos == 10 and order is SLOT:
                        sum_x1(u + 1)

            for i in range(NI):
                cross1(0, 0, 0, i, i, i)
            sum_x1(0)
            slot(0, 0, SLOT)
            slot(0, 1, SLOT)
            with dve.Fori(1, TILES - 1) as t:
                slot(t, 0, SLOT)
                slot(t, 1, SLOT)
            slot(TILES - 1, 0, SLOT)
            slot(TILES - 1, 1, LAST_SLOT)

        def mm(out, lhsT, rhs, start=True, stop=True):
            return nc.tensor.matmul(out, lhsT, rhs, start=start, stop=stop)

        @block.tensor
        def _(pe):
            def turn_x0(t):
                pe.wait_ge(gathered, 16 * F * (t + 1))
                after(pe, x0_copied, t)
                for i in range(NI):
                    last = nc.tensor.transpose(ps_x0[:, 128 * i:128 * (i + 1)],
                                               x0_rows[:, 128 * i:128 * (i + 1)], id_sb[:, :])
                last.then_inc(x0_turned, 1)

            def cross1(u, i, s, r):
                if i == 0:
                    after(pe, x1_copied, u)
                pe.wait_ge(z_ready, s + 1)
                for q in range(2):
                    m = mm(ps_x1[H * q:H * (q + 1), :], w0s_sb[:, i, :], Z[r][:, HALF * q:HALF * (q + 1)],
                           i == 0, i == NI - 1)
                m.then_inc(z_used, 1)

            def cross2(u, e, n, s, r):
                if n == 0:
                    after(pe, x2_copied, u - 1)
                pe.wait_ge(z_ready, s + 1)
                for q in range(2):
                    m = mm(ps_x2[e][H * q:H * (q + 1), :], w1_sb[:, n, :], Z[r][:, HALF * q:HALF * (q + 1)],
                           n == 0, n == NP2 - 1)
                m.then_inc(z_used, 1)

            def turn_x2(u):
                pe.wait_ge(x2_copied, u + 1)
                after(pe, x2r_copied, u)
                for k in range(KB):
                    last = nc.tensor.transpose(ps_x2r[:, 128 * k:128 * (k + 1)],
                                               x2_sb[:, 128 * k:128 * (k + 1)], id_sb[:, :])
                last.then_inc(x2_turned, 1)

            def turn_x0_blocks(u):
                pe.wait_ge(blocks_ready, u + 1)
                after(pe, diag_ready, u)
                pe.sem_inc(x0_turns_begun, 1)
                for k in range(2 * KB):
                    last = nc.tensor.transpose(ps_x0r[:, F * k:F * (k + 1)],
                                               x0_blocks[:, 128 * k:128 * (k + 1)], id_sb[0:F, 0:F])
                last.then_inc(x0r_turned, 1)

            def sum_g(u, e, q):
                if q == 0:
                    pe.wait_ge(x2r_copied, u + 1)
                    pe.wait_ge(diag_ready, u + 1)
                if not (isinstance(u, int) and u < 1):
                    pe.wait_ge(g_copied, 2 * u - 1 + q)
                for k in range(KB):
                    for par in range(2):
                        last = mm(ps_g[q][H * par:H * (par + 1), J3 * RB * k:J3 * RB * (k + 1)],
                                  x2_rows[:, k, H * q:H * (q + 1)],
                                  x0_diag[e][:, KB * q + k, par, :, :].rearrange("p j b -> p (j b)"))
                last.then_inc(g_summed, 1)

            def slot(t, e, order, back=True, front=False):
                u = 2 * t + e
                for pos, (kind, n) in enumerate(order):
                    s = NI + PER_SLOT * u + pos
                    r = (NI + pos) % ZR
                    if kind == "x1":
                        cross1(u + 1, n, s, r)
                        continue
                    cross2(u, e, n, s, r)
                    if front and n == (9 if e else 0):
                        turn_x0(t + 1 + e)
                    if back and n == 1:
                        turn_x2(u - 1)
                    if back and n in (3, 4):
                        sum_g(u - 1, 1 - e, n - 3)
                    if n == 5:
                        turn_x0_blocks(u)

            pe.wait_ge(ident_in, 16)
            turn_x0(0)
            pe.wait_ge(w0_ready, 1)
            for i in range(NI):
                cross1(0, i, i, i)
            pe.wait_ge(w1_in, 16)
            slot(0, 0, SLOT, back=False, front=True)
            pe.wait_ge(diag_fixed, 1)
            slot(0, 1, SLOT, front=True)
            with pe.Fori(1, TILES - 2) as t:
                slot(t, 0, SLOT)
                slot(t, 1, SLOT, front=True)
            slot(TILES - 2, 0, SLOT)
            slot(TILES - 2, 1, SLOT)
            slot(TILES - 1, 0, SLOT)
            slot(TILES - 1, 1, LAST_SLOT)
            turn_x2(UNITS - 1)
            for q in range(2):
                sum_g(UNITS - 1, 1, q)

            pe.wait_ge(tower_in, 16 * 8)
            pe.wait_ge(g_copied, 2 * UNITS)
            for j in range(F // 2):
                for half in range(2):
                    last = mm(ps_x1[H * (1 - half):H * (2 - half), :], w2_sb[:, j, :],
                              G[:, j, 512 * half:512 * (half + 1)], j == 0, j == F // 2 - 1)
            last.then_inc(z3_summed, 1)
            pe.wait_ge(z_ready2, 5)
            n = 0
            for half in range(2):
                cols = slice(512 * half, 512 * (half + 1))
                for m in range(M1 // 128):
                    if n >= 2:
                        pe.wait_ge(h1_ready, n - 1)
                    ps = ps_x2[n % 2]
                    mm(ps[:, :], wt1a_sb[:, 128 * m:128 * (m + 1)], z1_dense[:, cols], True, False)
                    mm(ps[:, :], wt1b_sb[:, 128 * m:128 * (m + 1)], z23[:, cols], False, True)\
                        .then_inc(h1_summed, 1)
                    n += 1
            n = 0
            for half in range(2):
                cols = slice(512 * half, 512 * (half + 1))
                pe.wait_ge(h1_ready, (half + 1) * (M1 // 128))
                for m in range(M2 // 128):
                    if n >= 2:
                        pe.wait_ge(h2_ready, n - 1)
                    for k in range(M1 // 128):
                        last = mm(ps_g[n % 2][:, :], wt2_sb[:, k, 128 * m:128 * (m + 1)], h1[k][:, cols],
                                  k == 0, k == M1 // 128 - 1)
                    last.then_inc(h2_summed, 1)
                    n += 1
            for half in range(2):
                cols = slice(512 * half, 512 * (half + 1))
                pe.wait_ge(h2_ready, 2 * (half + 1))
                ps = (ps_x2r, ps_x0r)[half]
                for k in range(M2 // 128):
                    last = mm(ps[0:1, :], wt3_sb[:, k:k + 1], h2[k][:, cols], k == 0, k == M2 // 128 - 1)
                last.then_inc(y_summed, 1)

        @block.scalar
        def _(act):
            def copy_x0(t):
                act.wait_ge(x0_turned, t + 1)
                after(act, x0_stored, X0_STORES * t)
                nc.scalar.copy(x0_cols[:, :, :].rearrange("p i b -> p (i b)"), ps_x0[:, 0:NI * TILE_ROWS])\
                    .then_inc(x0_copied, 1)

            def store_x0(t):
                act.wait_ge(x0_copied, t + 1)
                for i in range(NI + 1):
                    v = x0_dram[bass.ds(t, 1), :, FR * i:FR * (i + 1), :]\
                        .rearrange("t e f (d b) -> (t f d) e b", d=D)
                    src = x0_cols[:, i % NI, :].rearrange("p (e b) -> p e b", e=2)
                    act.dma_start(v, src).then_inc(x0_stored, 16)

            def complete_a(t, e):
                for i in range(NHALF):
                    act.wait_ge(A_in[e][i], 16 * (t + 1))
                    nc.scalar.copy(A[e][i][LOADED[1 - i], :], A[e][i][LOADED[i], :]).then_inc(A_ready, 1)

            def order_x0(u, t, e):
                act.wait_ge(x0_unit_in[e], 16 * (t + 1))
                after(act, x0r_turned, u)
                nc.scalar.copy(x0_blocks[:, :].rearrange("f (k d b) -> f k d b", d=D, b=RB),
                               x0_unit[e][:, :].rearrange("f (d k b) -> f k d b", d=D, b=RB))\
                    .then_inc(blocks_ready, 1)

            def copy_x1(u, t, e):
                act.wait_ge(z_used, NI if isinstance(u, int) and u == 0 else made(u - 1, ("x1", NI - 1)))
                if not (isinstance(u, int) and u < 1):
                    for j in range(NJ):
                        act.wait_ge(B_in[1 - e][j], 32 * (t + e))
                after(act, z1_ready, u)
                nc.scalar.copy(x1_sb[:, :], ps_x1[:, :]).then_inc(x1_copied, 1)

            def copy_x2(u, e, products):
                act.wait_ge(z_used, products)
                after(act, x2_turned, u)
                nc.scalar.copy(x2_sb[:, :].rearrange("p (k d b) -> p k d b", d=D, b=RB),
                               ps_x2[e][:, :].rearrange("p (d k b) -> p k d b", d=D, b=RB)).then_inc(x2_copied, 1)

            def copy_x2_rows(u):
                act.wait_ge(x2_turned, u + 1)
                after(act, g_summed, 2 * u)
                nc.scalar.copy(x2_rows[:, :, :].rearrange("p k n -> p (k n)"), ps_x2r[:, :])\
                    .then_inc(x2r_copied, 1)

            def spread_x0(u, e):
                act.wait_ge(x0r_turned, u + 1)
                after(act, g_summed, 2 * (u - 1))
                for b in range(RB):
                    last = nc.scalar.activation(
                        x0_diag[e][:, :, :, 0:F // 2, b].rearrange("p k a j -> p k j a"),
                        ps_x0r[:, 0:2 * KB * F].rearrange("p (k j a) -> p k j a", k=2 * KB, a=2),
                        ACT.Copy, scale=mask_sb[:, b:b + 1])
                last.then_inc(diag_ready, 1)

            def copy_g(u, q):
                act.wait_ge(g_summed, 2 * u + q + 1)
                nc.scalar.copy(
                    G[:, :, bass.ds(q * (BATCH // 2) + u * ROWS_Q, ROWS_Q)].rearrange("p j (k b) -> p k j b", b=RB),
                    ps_g[q][:, 0:KB * J3 * RB].rearrange("p (k j b) -> p k j b", k=KB, j=J3))\
                    .then_inc(g_copied, 1)

            def slot(t, e, back=True, front=False, ahead=2):
                u = 2 * t + e
                if back:
                    copy_x2(u - 1, 1 - e, made(u - 1, ("x2", NP2 - 1)))
                if e == 0 and front:
                    copy_x0(1)
                    store_x0(1)
                if back:
                    copy_x2_rows(u - 1)
                order_x0(u, t, e)
                if ahead > 0:
                    copy_x1(u + 1, t + e, 1 - e)
                if back:
                    copy_g(u - 1, 0)
                    copy_g(u - 1, 1)
                spread_x0(u, e)
                if e == 1 and front:
                    copy_x0(t + 2)
                if ahead > 1:
                    complete_a(t + 1, e)
                if e == 1 and front:
                    store_x0(t + 2)

            copy_x0(0)
            store_x0(0)
            complete_a(0, 0)
            copy_x1(0, 0, 0)
            complete_a(0, 1)
            act.wait_ge(mask_in, 16)
            slot(0, 0, back=False, front=True)
            slot(0, 1, front=True)
            with act.Fori(1, TILES - 2) as t:
                slot(t, 0)
                slot(t, 1, front=True)
            slot(TILES - 2, 0)
            slot(TILES - 2, 1)
            slot(TILES - 1, 0, ahead=1)
            slot(TILES - 1, 1, ahead=0)
            copy_x2(UNITS - 1, 1, NI + PER_SLOT * UNITS - NI)
            copy_x2_rows(UNITS - 1)
            copy_g(UNITS - 1, 0)
            copy_g(UNITS - 1, 1)

            act.wait_ge(z1_ready, UNITS)
            act.wait_ge(tower_in, 16 * 8)
            act.wait_ge(g_copied, 2 * UNITS)
            for q in range(2):
                nc.scalar.copy(z1_dense[0:H, 512 * q:512 * (q + 1)], z1_q[H * q:H * (q + 1), :])\
                    .then_inc(z_ready2, 1)
            nc.scalar.copy(z23[0:H, :], G[0:H, J3 - 1, :]).then_inc(z_ready2, 1)
            act.wait_ge(z3_summed, 1)
            for half in range(2):
                nc.scalar.copy(z23[H:2 * H, 512 * half:512 * (half + 1)],
                               ps_x1[H * (1 - half):H * (2 - half), :]).then_inc(z_ready2, 1)
            n = 0
            for half in range(2):
                for m in range(M1 // 128):
                    act.wait_ge(h1_summed, n + 1)
                    nc.scalar.activation(h1[m][:, 512 * half:512 * (half + 1)], ps_x2[n % 2][:, :], ACT.Relu,
                                         bias=bt1_sb[:, m:m + 1]).then_inc(h1_ready, 1)
                    n += 1
            n = 0
            for half in range(2):
                for m in range(M2 // 128):
                    act.wait_ge(h2_summed, n + 1)
                    nc.scalar.activation(h2[m][:, 512 * half:512 * (half + 1)], ps_g[n % 2][:, :], ACT.Relu,
                                         bias=bt2_sb[:, m:m + 1]).then_inc(h2_ready, 1)
                    n += 1
            for half in range(2):
                act.wait_ge(y_summed, half + 1)
                nc.scalar.copy(y_sb[:, 512 * half:512 * (half + 1)], (ps_x2r, ps_x0r)[half][0:1, :])\
                    .then_inc(y_ready, 1)


def kernel(**inputs):
    import numpy as np
    import concourse.bacc as bacc
    from concourse import mybir as mb
    from concourse.bass_utils import run_bass_kernel_spmd

    a = {k: np.asarray(v) for k, v in inputs.items()}
    w0 = a["L0_rec_W0"].reshape(F, F, H)
    w0a = np.zeros((HR, FR, NI, H), w0.dtype)
    w0b = np.zeros((HR, FR, NI, H), w0.dtype)
    for i in range(NI):
        for g in range(HR):
            w0a[g, :, i] = w0[FR * i:FR * (i + 1), (FR * i + g) % F]
            if g >= FR:
                w0b[g, :, i] = w0[(FR * i + g) % F, FR * i:FR * (i + 1)]
    w1 = a["L0_rec_W1"].reshape(NI, FR, NJ, HR, H).transpose(3, 1, 0, 2, 4)
    w2 = a["L0_rec_W2"].reshape(F // 2, 128, H).transpose(1, 0, 2)
    wt1 = a["W_top1"]
    arrays = {
        "dense_t": a["dense_ctx"].reshape(TILES, 2, 2, ROWS_Q, DENSE).transpose(4, 2, 0, 1, 3).reshape(DENSE, BATCH),
        "ids": a["ids"].reshape(TILES, 128, F).transpose(1, 0, 2).reshape(128, TILES * F),
        "w0a": w0a.reshape(128, NI, H),
        "w0b": w0b.reshape(128, NI, H),
        "w1": w1.reshape(128, NP2, H),
        "w2": w2,
        "wt1_z1_dense": np.concatenate([wt1[0:H], wt1[3 * H:]], axis=0),
        "wt1_z2_z3": wt1[H:3 * H],
        "bt1": a["b_top1"].reshape(M1 // 128, 128).transpose(1, 0),
        "wt2": a["W_top2"].reshape(M1 // 128, 128, M2).transpose(1, 0, 2),
        "bt2": a["b_top2"].reshape(M2 // 128, 128).transpose(1, 0),
        "wt3": a["W_top3"].reshape(M2 // 128, 128).transpose(1, 0),
        "ident": np.eye(128, dtype=np.float32),
        "mask": np.tile(np.eye(RB, dtype=np.float32), (128 // RB, 1)),
    }
    for f in range(F):
        arrays[f"tbl_{f}"] = a[f"tbl_{f}"]
    nc = bacc.Bacc("TRN2", target_bir_lowering=False, num_devices=1)
    arrays = {k: np.ascontiguousarray(v) for k, v in arrays.items()}
    ap = {k: nc.dram_tensor(k, v.shape, mb.dt.from_np(v.dtype), kind="ExternalInput").ap()
          for k, v in arrays.items()}
    out = nc.dram_tensor("y", (1, BATCH), F32, kind="ExternalOutput").ap()
    cin_tower(nc, ap["dense_t"], ap["ids"], [ap[f"tbl_{f}"] for f in range(F)], ap["w0a"], ap["w0b"],
              ap["w1"], ap["w2"], (ap["wt1_z1_dense"], ap["wt1_z2_z3"]), ap["bt1"], ap["wt2"], ap["bt2"],
              ap["wt3"], ap["ident"], ap["mask"], out)
    y = run_bass_kernel_spmd(nc, [arrays], core_ids=[0]).results[0]["y"]
    return y.reshape(2, TILES, 2, ROWS_Q).transpose(1, 2, 0, 3).reshape(BATCH, 1)
```

```python
from contextlib import ExitStack

import concourse.bass as bass
from concourse import mybir

F32 = mybir.dt.float32
ALU = mybir.AluOpType
ACT = mybir.ActivationFunctionType
AX = mybir.AxisListType

BATCH, F, D, H, DENSE = 1024, 24, 16, 64, 16
M1, M2 = 512, 256
TILE_ROWS = 128
TILES = BATCH // TILE_ROWS
UNITS = 2 * TILES
W = 4
GROUPS = UNITS // W
COLS = TILE_ROWS * D // 2
HALF = COLS // 2
RB = 8
ROWS_U = TILE_ROWS // 2
KB = HALF // 128
FR, HR = 8, 16
NI, NJ = F // FR, H // HR
NP2 = NI * NJ
J3 = F // 2 + 1
ROWS_Q = KB * RB
GQ = W * ROWS_Q
GROWS = 2 * GQ
NHALF = 2
LOADED = [slice(0, 64), slice(64, 128), slice(0, 128)]
QUARTERS = 4
SETS = 2
ZR = 5

BEFORE = 2
SLOT = [("x2", n) for n in range(BEFORE)] + [("x1", i) for i in range(NI)] + \
       [("x2", n) for n in range(BEFORE, NP2)]
WARM = (20, 40, 10, 8, 40)
LAST_SLOT = [s for s in SLOT if s[0] == "x2"]
X0_STORES = 16 * 3
PER_SLOT = len(SLOT)
POS = {s: n for n, s in enumerate(SLOT)}
assert PER_SLOT % ZR == 0


def diag_block(k):
    return QUARTERS * (k % 2) + k // 2


def made(u, what):
    return NI + PER_SLOT * u + POS[what] + 1


def cin_tower(nc, dense_t, ids, tables, small_ids, small_tables, small_rows, chunks, w0a, w0b, w1, w2, wt1, bt1, wt2, bt2, wt3, ident, mask, out):
    x0_dram = nc.dram_tensor("x0_scratch", [TILES, 2, F + FR, COLS], F32, kind="Internal").ap()

    CR = small_tables.shape[0]
    HOT = [(k, c) for k in range(SETS) for c in range(chunks[k])]

    ctx = ExitStack()
    with ctx:
        def sb(name, shape, dt=F32):
            return ctx.enter_context(nc.sbuf_tensor(name, shape, dt))

        def bank(name):
            return ctx.enter_context(nc.psum_tensor(name, [128, 512], F32))

        def sem(name):
            return ctx.enter_context(nc.semaphore(name))

        ids_sb = sb("ids_sb", [128, TILES * F], mybir.dt.int32)
        ids_tile = sb("ids_tile", [128, F], mybir.dt.int32)
        id_sb = sb("id_sb", [128, 128])
        mask_sb = sb("mask_sb", [128, RB])
        w0_sb = sb("w0_sb", [128, NI, H])
        w0m_sb = sb("w0m_sb", [128, NI, H])
        w0s_sb = sb("w0s_sb", [128, NI, H])
        w1_sb = sb("w1_sb", [128, NP2, H])
        w2_sb = sb("w2_sb", [128, F // 2, H])
        wt1a_sb = sb("wt1a_sb", [H + DENSE, M1])
        wt1b_sb = sb("wt1b_sb", [2 * H, M1])
        wt2_sb = sb("wt2_sb", [128, M1 // 128, M2])
        wt3_sb = sb("wt3_sb", [128, M2 // 128])
        bt1_sb = sb("bt1_sb", [128, M1 // 128])
        bt2_sb = sb("bt2_sb", [128, M2 // 128])
        small_sb = sb("small_sb", [CR, len(HOT), FR, D])
        small_rows_sb = sb("small_rows_sb", [CR, max(chunks)])
        small_ids_sb = [sb(f"small_ids_sb{k}", [CR, FR * TILE_ROWS], mybir.dt.int32) for k in range(SETS)]
        small_ids_f32 = [sb(f"small_ids_f32_{k}", [CR, FR * TILE_ROWS]) for k in range(SETS)]
        x0_small = [[sb(f"x0_small{k}{g}", [D, FR // 4, TILE_ROWS]) for g in range(4)] for k in range(SETS)]
        x0_rows = sb("x0_rows", [128, F * D])
        x0_cols = sb("x0_cols", [128, NI, TILE_ROWS])
        x0_blocks = sb("x0_blocks", [128, 2, 128])
        A = [[sb(f"A{e}{i}", [128, COLS]) for i in range(NI)] for e in range(2)]
        B = [[sb(f"B{e}{j}", [128, COLS]) for j in range(NJ)] for e in range(2)]
        C = [sb(f"C{i}", [128, COLS]) for i in range(NI)]
        Z = [sb(f"Z{r}", [128, COLS]) for r in range(ZR)]
        x0_unit = [sb(f"x0_unit{e}", [128, COLS // 4]) for e in range(2)]
        x1_sb = sb("x1_sb", [128, HALF])
        x2_sb = sb("x2_sb", [128, HALF])
        x2_rows = sb("x2_rows", [128, KB, 128])
        x0_diag = [sb(f"x0_diag{e}", [128, 2 * KB, 2, J3, RB]) for e in range(2)]
        G = sb("G", [128, J3, GROWS])
        z1_q = sb("z1_q", [128, BATCH // 2])
        dense_sb = sb("dense_sb", [DENSE, BATCH])
        z1_dense = sb("z1_dense", [H + DENSE, GROWS])
        z23 = sb("z23", [128, GROWS])
        h1 = [sb(f"h1_{m}", [128, GROWS]) for m in range(M1 // 128)]
        h2 = [sb(f"h2_{m}", [128, GROWS]) for m in range(M2 // 128)]
        y_sb = sb("y_sb", [1, BATCH])

        ps_x2 = [bank(f"ps_x2{e}") for e in range(2)]
        ps_x1 = bank("ps_x1")
        ps_x2r = bank("ps_x2r")
        ps_g = [bank(f"ps_g{q}") for q in range(2)]
        ps_x0 = bank("ps_x0")
        ps_x0r = ps_x0
        ps_tower = bank("ps_tower")
        ps_small = [ps_g, ps_x2]

        ids_in = sem("ids_in")
        small_rows_in = sem("small_rows_in")
        small_in = [sem(f"small_in{k}") for k in range(SETS)]
        small_ids_in = [sem(f"small_ids_in{k}") for k in range(SETS)]
        gathered = [sem(f"gathered{i}") for i in range(NI)]
        ident_in, mask_in, w0_in, w1_in, tower_in = (sem(n) for n in (
            "ident_in", "mask_in", "w0_in", "w1_in", "tower_in"))
        A_in = [[sem(f"A_in{e}{i}") for i in range(NI)] for e in range(2)]
        B_in = [[sem(f"B_in{e}{j}") for j in range(NJ)] for e in range(2)]
        C_in = [sem(f"C_in{i}") for i in range(NI)]
        C_early = [sem(f"C_early{i}") for i in range(1, NI)]
        x0_unit_in = [sem(f"x0_unit_in{e}") for e in range(2)]
        x0_stored, y_stored = sem("x0_stored"), sem("y_stored")
        part_stored = [sem(f"part_stored{i}") for i in range(NI)]
        small_stored = sem("small_stored")
        ids_ready = sem("ids_ready")
        gathers_begun = sem("gathers_begun")
        x0_turned = sem("x0_turned")
        hot_used = sem("hot_used")
        z_used = sem("z_used")
        x2_turned, x0r_turned = sem("x2_turned"), sem("x0r_turned")
        g_summed = sem("g_summed")
        z3_summed, h1_summed, h2_summed, y_summed = (sem(n) for n in (
            "z3_summed", "h1_summed", "h2_summed", "y_summed"))
        x0_copied, x1_copied, x2_copied, x2r_copied = (sem(n) for n in (
            "x0_copied", "x1_copied", "x2_copied", "x2r_copied"))
        small_copied = sem("small_copied")
        blocks_ready, diag_ready, g_copied = sem("blocks_ready"), sem("diag_ready"), sem("g_copied")
        A_ready = sem("A_ready")
        z12_ready, z3_ready, h1_ready, h2_ready, y_ready = (sem(n) for n in (
            "z12_ready", "z3_ready", "h1_ready", "h2_ready", "y_ready"))
        z_ready = sem("z_ready")
        z1_ready = sem("z1_ready")
        w0_ready = sem("w0_ready")
        small_ids_ready, hot_ready = sem("small_ids_ready"), sem("hot_ready")
        diag_fixed = sem("diag_fixed")

        def after(engine, semaphore, count):
            if not isinstance(count, int) or count > 0:
                engine.wait_ge(semaphore, count)

        def store_small(engine, k, e, stored, groups=range(4)):
            for g in groups:
                engine.wait_ge(small_copied, 2 * (4 * k + g + 1))
                v = x0_dram[0:1, e, FR * (k + 1) + g:FR * (k + 2):4, :].rearrange("t f (d b) -> (t d) f b", d=D)
                engine.dma_start(v, x0_small[k][g][:, :, ROWS_U * e:ROWS_U * (e + 1)]).then_inc(stored, 16)

        block = ctx.enter_context(nc.Block())

        @block.gpsimd
        def _(pool):
            pool.dma_start(ids_sb[:, :], ids).then_inc(ids_in, 16)
            pool.wait_ge(ids_in, 16)

            def gather(ids_of, f):
                pool.indirect_dma_start(
                    out=x0_rows[:, f * D:(f + 1) * D], out_offset=None, in_=tables[f],
                    in_offset=bass.IndirectOffsetOnAxis(ap=ids_of[:, f:f + 1], axis=0),
                ).then_inc(gathered[f // FR], 16)

            for f in range(FR):
                gather(ids_sb, f)
            for f in [*range(FR, F), *range(FR)]:
                if f == 0:
                    pool.wait_ge(x0_turned, 1)
                gather(ids_sb[:, F:2 * F], f)
            with pool.Fori(2, TILES) as t:
                pool.wait_ge(x0_turned, t)
                pool.tensor_copy(ids_tile[:, :], ids_sb[:, bass.ds(t * F, F)]).then_inc(ids_ready, 1)
                pool.wait_ge(ids_ready, t - 1)
                pool.sem_inc(gathers_begun, 1)
                for f in range(F):
                    gather(ids_tile, f)

        @block.sync
        def _(sp):
            sp.dma_start(id_sb[:, :], ident).then_inc(ident_in, 16)
            sp.dma_start(small_rows_sb[:, :], small_rows).then_inc(small_rows_in, 16)
            for k in range(SETS):
                src = small_ids[k:k + 1, :].to_broadcast([CR, FR * TILE_ROWS])
                sp.dma_start(small_ids_sb[k][:, :], src).then_inc(small_ids_in[k], 16)
                at = slice(sum(chunks[:k]), sum(chunks[:k + 1]))
                sp.dma_start(small_sb[:, at, :, :], small_tables[:, at, :, :]).then_inc(small_in[k], 16)
            sp.dma_start(w0_sb[:, :, :], w0a).then_inc(w0_in, 16)
            sp.dma_start(w0m_sb[:, :, :], w0b).then_inc(w0_in, 16)
            sp.dma_start(mask_sb[:, :], mask).then_inc(mask_in, 16)
            sp.dma_start(w1_sb[:, :, :], w1).then_inc(w1_in, 16)
            for dst, src in ((w2_sb[:, :, :], w2), (wt1a_sb[:, :], wt1[0]), (wt1b_sb[:, :], wt1[1]),
                             (wt2_sb[:, :, :], wt2), (wt3_sb[:, :], wt3), (bt1_sb[:, :], bt1),
                             (bt2_sb[:, :], bt2), (dense_sb[:, :], dense_t)):
                sp.dma_start(dst, src).then_inc(tower_in, 16)

            def load_a(t, e, i):
                src = x0_dram[bass.ds(t, 1), e, FR * i:FR * (i + 1), :]
                p = LOADED[i]
                sp.dma_start(A[e][i][p, :], src.to_broadcast([(p.stop - p.start) // FR, FR, COLS]))\
                    .then_inc(A_in[e][i], 16)

            def load_c(t, e, i):
                src = x0_dram[bass.ds(t, 1), e, FR * i:FR * i + HR, :].rearrange("t f c -> (t f) c")
                sp.dma_start(C[i][:, :], src.unsqueeze(1).to_broadcast([HR, FR, COLS])).then_inc(C_in[i], 16)

            def load_c_half(i, h, loaded):
                at = FR * (i + h)
                src = x0_dram[0:1, 0, at:at + FR, :].rearrange("t f c -> (t f) c")
                sp.dma_start(C[i][64 * h:64 * (h + 1), :], src.unsqueeze(1).to_broadcast([HR // 2, FR, COLS]))\
                    .then_inc(loaded, 16)

            def load_b(u, e, js=range(NJ)):
                sp.wait_ge(x1_copied, u + 1)
                for j in js:
                    for q in range(2):
                        src = x1_sb[H * q + HR * j:H * q + HR * (j + 1), :].unsqueeze(1)
                        sp.dma_start(B[e][j][:, HALF * q:HALF * (q + 1)], src.to_broadcast([HR, FR, HALF]))\
                            .then_inc(B_in[e][j], 16)

            def load_x0_unit(t, e):
                src = x0_dram[bass.ds(t, 1), e, :, :]
                v = src.rearrange("t f (d h b) -> h (t f) d b", d=D, h=QUARTERS)
                sp.dma_start(x0_unit[e][:, :], v).then_inc(x0_unit_in[e], 16)

            store_small(sp, 0, 1, small_stored)
            sp.wait_ge(part_stored[1], 16 * 4)
            load_a(0, 0, 1)
            load_c_half(1, 0, C_early[0])
            sp.wait_ge(part_stored[0], 32)
            load_a(0, 0, 0)
            load_c(0, 0, 0)
            store_small(sp, 1, 0, part_stored[2], (2, 3))
            load_c_half(2, 1, C_early[1])
            sp.wait_ge(part_stored[2], 16 * 4)
            load_c_half(1, 1, C_in[1])
            load_c_half(2, 0, C_in[2])
            load_a(0, 0, 2)
            store_small(sp, 1, 1, small_stored)
            load_a(0, 1, 0)
            sp.wait_ge(small_stored, 16 * 4 * SETS)
            load_a(0, 1, 1)
            sp.wait_ge(z_ready, 1)
            load_c(0, 1, 0)
            load_a(0, 1, 2)
            load_b(0, 0, (0, 1))
            sp.wait_ge(z_ready, NI)
            load_c(0, 1, 1)
            load_c(0, 1, 2)
            load_b(0, 0, (2, 3))
            load_x0_unit(0, 0)
            load_x0_unit(0, 1)

            def load_c_next(t, e, i):
                sp.wait_ge(z_ready, made(2 * t + e - 2, ("x1", i)))
                load_c(t, e, i)

            def load_a_next(t, e, i):
                sp.wait_ge(z_ready, made(2 * t + e - 2, ("x2", NJ * (i + 1) - 1)))
                load_a(t, e, i)

            def load_x0_unit_next(t, e):
                sp.wait_ge(blocks_ready, 2 * t + e - 1)
                load_x0_unit(t, e)

            def load_unit(t, e):
                if e == 0:
                    sp.wait_ge(x0_stored, X0_STORES * t)
                for i in range(NI):
                    load_c_next(t, e, i)
                load_b(2 * t + e - 1, 1 - e)
                load_a_next(t, e, 0)
                load_a_next(t, e, 1)
                load_a_next(t, e, 2)
                load_x0_unit_next(t, e)

            sp.wait_ge(x0_stored, X0_STORES)
            load_a_next(1, 0, 0)
            load_c_next(1, 0, 0)
            load_c_next(1, 0, 1)
            load_b(1, 1, (0, 1))
            load_a_next(1, 0, 1)
            load_c_next(1, 0, 2)
            load_a_next(1, 0, 2)
            load_b(1, 1, (2, 3))
            load_x0_unit_next(1, 0)
            load_unit(1, 1)
            with sp.Fori(2, TILES) as t:
                for e in range(2):
                    load_unit(t, e)
            load_b(UNITS - 1, 1)
            sp.wait_ge(y_ready, GROUPS)
            sp.dma_start(out, y_sb[:, :]).then_inc(y_stored, 16)
            sp.wait_ge(y_stored, 16)

        @block.vector
        def _(dve):
            dve.wait_ge(small_rows_in, 16)
            for n, (k, c) in enumerate(HOT):
                if c == 0:
                    dve.wait_ge(small_ids_in[k], 16)
                    nc.vector.tensor_copy(small_ids_f32[k][:, :], small_ids_sb[k][:, :]).then_inc(small_ids_ready, 1)
                    dve.wait_ge(small_ids_ready, k + 1)
                if n >= ZR:
                    dve.wait_ge(hot_used, n - ZR + 1)
                nc.vector.tensor_scalar(Z[n % ZR][0:CR, :], small_ids_f32[k][:, :], small_rows_sb[:, c:c + 1],
                                        None, ALU.is_equal).then_inc(hot_ready, 1)
            dve.wait_ge(mask_in, 16)
            for e in range(2):
                for k in range(2 * KB):
                    nc.vector.tensor_copy(x0_diag[e][:, k, 0, J3 - 1, :], mask_sb[:, :])
                last = nc.vector.memset(x0_diag[e][:, :, 1, J3 - 1, :], 0.0)
            last.then_inc(diag_fixed, 1)
            dve.wait_ge(w0_in, 32)
            nc.vector.tensor_tensor(w0s_sb[:, :, :], w0_sb[:, :, :], w0m_sb[:, :, :], ALU.add)\
                .then_inc(w0_ready, 1)

            def by_d(x):
                return x[:, :].rearrange("p (d q b) -> p q d b", d=D, q=2)

            def by_q(x):
                return x[:, :].rearrange("p (q d b) -> p q d b", d=D, q=2)

            def product(s):
                after(dve, z_used, s - ZR + 1)

            def cross1(u, t, e, i, s, r):
                if i < NHALF:
                    dve.wait_ge(A_ready, NHALF * u + i + 1)
                else:
                    dve.wait_ge(A_in[e][i], 16 * (t + 1))
                dve.wait_ge(C_in[i], 16 * (u + 1))
                product(s)
                nc.vector.tensor_tensor(by_q(Z[r]), by_d(A[e][i]), by_d(C[i]), ALU.mult)\
                    .then_inc(z_ready, 1)

            def cross2(t, e, n, s, r):
                i, j = n // NJ, n % NJ
                if i == 0:
                    dve.wait_ge(B_in[e][j], 32 * (t + 1))
                product(s)
                nc.vector.tensor_tensor(by_q(Z[r]), by_d(A[e][i]), by_q(B[e][j]), ALU.mult)\
                    .then_inc(z_ready, 1)

            def sum_x1(u):
                dve.wait_ge(x1_copied, u + 1)
                nc.vector.tensor_reduce(
                    z1_q[:, bass.ds(u * ROWS_Q, ROWS_Q)],
                    x1_sb[:, :].rearrange("p (d b) -> p b d", d=D), AX.X, ALU.add)\
                    .then_inc(z1_ready, 1)

            def slot(t, e, order):
                u = 2 * t + e
                for pos, (kind, n) in enumerate(order):
                    s = NI + PER_SLOT * u + pos
                    r = (NI + pos) % ZR
                    if kind == "x1":
                        cross1(u + 1, t + e, 1 - e, n, s, r)
                    else:
                        cross2(t, e, n, s, r)
                    if pos == 10 and order is SLOT:
                        sum_x1(u + 1)

            dve.wait_ge(hot_used, len(HOT))
            for i in range(NI):
                if i > 0:
                    dve.wait_ge(C_early[i - 1], 16)
                cross1(0, 0, 0, i, i, i)
            sum_x1(0)
            slot(0, 0, SLOT)
            slot(0, 1, SLOT)
            with dve.Fori(1, TILES - 1) as t:
                slot(t, 0, SLOT)
                slot(t, 1, SLOT)
            slot(TILES - 1, 0, SLOT)
            slot(TILES - 1, 1, LAST_SLOT)

        def mm(out, lhsT, rhs, start=True, stop=True):
            return nc.tensor.matmul(out, lhsT, rhs, start=start, stop=stop)

        @block.tensor
        def _(pe):
            def turn_x0_part(t, i):
                pe.wait_ge(gathered[i], 16 * FR * (t + 1 if i == 0 else t))
                return nc.tensor.transpose(ps_x0[:, 128 * i:128 * (i + 1)],
                                           x0_rows[:, 128 * i:128 * (i + 1)], id_sb[:, :])

            def turn_x0(t, spread):
                pe.wait_ge(x0_copied, t)
                after(pe, diag_ready, spread)
                for i in range(NI):
                    last = turn_x0_part(t, i)
                last.then_inc(x0_turned, 1)

            def keep_warm(n):
                for _ in range(n):
                    nc.tensor.transpose(ps_tower[:, 0:128], id_sb[:, :], id_sb[:, :])

            def cross1(u, i, s, r):
                if i == 0:
                    after(pe, x1_copied, u)
                pe.wait_ge(z_ready, s + 1)
                for q in range(2):
                    m = mm(ps_x1[H * q:H * (q + 1), :], w0s_sb[:, i, :], Z[r][:, HALF * q:HALF * (q + 1)],
                           i == 0, i == NI - 1)
                m.then_inc(z_used, 1)

            def cross2(u, e, n, s, r):
                if n == 0:
                    after(pe, x2_copied, u - 1)
                pe.wait_ge(z_ready, s + 1)
                for q in range(2):
                    m = mm(ps_x2[e][H * q:H * (q + 1), :], w1_sb[:, n, :], Z[r][:, HALF * q:HALF * (q + 1)],
                           n == 0, n == NP2 - 1)
                m.then_inc(z_used, 1)

            def turn_x2(u):
                pe.wait_ge(x2_copied, u + 1)
                after(pe, x2r_copied, u)
                for k in range(KB):
                    last = nc.tensor.transpose(ps_x2r[:, 128 * k:128 * (k + 1)],
                                               x2_sb[:, 128 * k:128 * (k + 1)], id_sb[:, :])
                last.then_inc(x2_turned, 1)

            def turn_x0_blocks(u, tiles_turned):
                pe.wait_ge(blocks_ready, u + 1)
                pe.wait_ge(x0_copied, tiles_turned)
                after(pe, diag_ready, u)
                for k in range(2):
                    last = nc.tensor.transpose(ps_x0r[:, 128 * k:128 * (k + 1)], x0_blocks[:, k, :], id_sb[:, :])
                last.then_inc(x0r_turned, 1)

            def sum_g(u, e, q):
                if q == 0:
                    pe.wait_ge(x2r_copied, u + 1)
                    pe.wait_ge(diag_ready, u + 1)
                if not (isinstance(u, int) and u < 1):
                    pe.wait_ge(g_copied, 2 * u - 1 + q)
                for k in range(KB):
                    for par in range(2):
                        last = mm(ps_g[q][H * par:H * (par + 1), J3 * RB * k:J3 * RB * (k + 1)],
                                  x2_rows[:, k, H * q:H * (q + 1)],
                                  x0_diag[e][:, diag_block(KB * q + k), par, :, :].rearrange("p j b -> p (j b)"))
                last.then_inc(g_summed, 1)

            def sum_z3(g, js=range(F // 2)):
                if js[0] == 0:
                    pe.wait_ge(g_copied, 2 * W * (g + 1))
                    after(pe, y_ready, g)
                for j in js:
                    for q in range(2):
                        last = mm(ps_tower[H * (1 - q):H * (2 - q), 0:GQ], w2_sb[:, j, :],
                                  G[:, j, GQ * q:GQ * (q + 1)], j == 0, j == F // 2 - 1)
                if js[-1] == F // 2 - 1:
                    last.then_inc(z3_summed, 1)

            def sum_h1(g, m, banks=(ps_tower,)):
                if m == 0:
                    pe.wait_ge(z12_ready, 4 * (g + 1))
                    pe.wait_ge(z3_ready, 2 * (g + 1))
                if m >= len(banks):
                    pe.wait_ge(h1_ready, M1 // 128 * g + m + 1 - len(banks))
                ps = banks[m % len(banks)][:, 0:GROWS]
                mm(ps, wt1a_sb[:, 128 * m:128 * (m + 1)], z1_dense[:, :], True, False)
                mm(ps, wt1b_sb[:, 128 * m:128 * (m + 1)], z23[:, :], False, True).then_inc(h1_summed, 1)

            def sum_h2(g, m, banks=(ps_tower,)):
                pe.wait_ge(h1_ready, M1 // 128 * (g + 1))
                if m >= len(banks):
                    pe.wait_ge(h2_ready, M2 // 128 * g + m + 1 - len(banks))
                for k in range(M1 // 128):
                    last = mm(banks[m % len(banks)][:, 0:GROWS], wt2_sb[:, k, 128 * m:128 * (m + 1)],
                              h1[k][:, :], k == 0, k == M1 // 128 - 1)
                last.then_inc(h2_summed, 1)

            def sum_y(g):
                pe.wait_ge(h2_ready, M2 // 128 * (g + 1))
                for k in range(M2 // 128):
                    last = mm(ps_tower[0:1, 0:GROWS], wt3_sb[:, k:k + 1], h2[k][:, :], k == 0, k == M2 // 128 - 1)
                last.then_inc(y_summed, 1)

            def tower(g, w, n):
                if w == 0 and n in (8, 9, 10):
                    at = 4 * (n - 8)
                    sum_z3(g, range(at, at + F // 6))
                if w == 1 and n in (2, 5, 8):
                    sum_h1(g, n // 3)
                if (w, n) == (2, 2):
                    sum_h1(g, 3)
                if (w, n) == (2, 8):
                    sum_h2(g, 0)
                if (w, n) == (3, 2):
                    sum_h2(g, 1)
                if (w, n) == (3, 7):
                    sum_y(g)

            def slot(g, w, order, back=True, front=False, towers=True):
                t, e = 2 * g + w // 2, w % 2
                u = W * g + w
                turned = min(t + 2, TILES) if isinstance(t, int) else t + 2
                for pos, (kind, n) in enumerate(order):
                    s = NI + PER_SLOT * u + pos
                    r = (NI + pos) % ZR
                    if kind == "x1":
                        cross1(u + 1, n, s, r)
                        continue
                    cross2(u, e, n, s, r)
                    if back and n == 1:
                        turn_x2(u - 1)
                    if n == 2:
                        turn_x0_blocks(u, turned)
                    if back and n in (3, 4):
                        sum_g(u - 1, 1 - e, n - 3)
                    if towers:
                        tower(g - 1, w, n)
                    if isinstance(u, int) and u == 0 and n == 1:
                        turn_x0(1, 0)
                    if front and e and n == 6:
                        turn_x0(t + 2, u + 1)

            pe.wait_ge(ident_in, 16)
            keep_warm(WARM[0])
            for n, (k, c) in enumerate(HOT):
                if c == 0:
                    pe.wait_ge(small_in[k], 16)
                pe.wait_ge(hot_ready, n + 1)
                for f in range(FR):
                    g, half = f % 4, f // 4
                    last = mm(ps_small[k][half][32 * g:32 * g + D, 0:TILE_ROWS], small_sb[:, n, f, :],
                              Z[n % ZR][0:CR, TILE_ROWS * f:TILE_ROWS * (f + 1)], c == 0, c == chunks[k] - 1)
                last.then_inc(hot_used, 1)
                if (k, c) == (1, 4):
                    turn_x0_part(0, 0).then_inc(x0_turned, 1)
            pe.wait_ge(w0_ready, 1)
            keep_warm(WARM[1])
            for i in range(NI):
                cross1(0, i, i, i)
                keep_warm(WARM[2 + i])
            pe.wait_ge(w1_in, 16)
            for w in range(W):
                slot(0, w, SLOT, back=w > 0, front=w in (1, 3), towers=False)
                if w == 0:
                    pe.wait_ge(diag_fixed, 1)
            pe.wait_ge(tower_in, 16 * 8)
            with pe.Fori(1, GROUPS - 1) as g:
                for w in range(W):
                    slot(g, w, SLOT, front=w in (1, 3))
            for w in range(W):
                slot(GROUPS - 1, w, LAST_SLOT if w == W - 1 else SLOT)
            turn_x2(UNITS - 1)
            for q in range(2):
                sum_g(UNITS - 1, 1, q)
            sum_z3(GROUPS - 1)
            for m in range(M1 // 128):
                sum_h1(GROUPS - 1, m, (ps_tower, ps_x0))
            for m in range(M2 // 128):
                sum_h2(GROUPS - 1, m, (ps_tower, ps_x0))
            sum_y(GROUPS - 1)

        @block.scalar
        def _(act):
            def copy_x0(t):
                act.wait_ge(x0_turned, t + 1)
                after(act, x0_stored, X0_STORES * (t - 1))
                if isinstance(t, int) and t == 1:
                    act.wait_ge(part_stored[0], 32)
                nc.scalar.copy(x0_cols[:, :, :].rearrange("p i b -> p (i b)"), ps_x0[:, 0:NI * TILE_ROWS])\
                    .then_inc(x0_copied, 1)

            def store_x0_part(t, i, stored):
                v = x0_dram[bass.ds(t, 1), :, FR * i:FR * (i + 1), :]\
                    .rearrange("t e f (d b) -> (t f d) e b", d=D)
                src = x0_cols[:, i % NI, :].rearrange("p (e b) -> p e b", e=2)
                act.dma_start(v, src).then_inc(stored, 16)

            def store_x0(t):
                act.wait_ge(x0_copied, t + 1)
                for e in range(2):
                    v = x0_dram[bass.ds(t, 1), e, 0:F, :].rearrange("t (i f) (d b) -> (t f d) i b", d=D, i=NI)
                    act.dma_start(v, x0_cols[:, :, ROWS_U * e:ROWS_U * (e + 1)]).then_inc(x0_stored, 16)
                store_x0_part(t, NI, x0_stored)

            def complete_a(t, e):
                for i in range(NHALF):
                    act.wait_ge(A_in[e][i], 16 * (t + 1))
                    nc.scalar.copy(A[e][i][LOADED[1 - i], :], A[e][i][LOADED[i], :]).then_inc(A_ready, 1)

            def order_x0(u, t, e):
                act.wait_ge(x0_unit_in[e], 16 * (t + 1))
                after(act, x0r_turned, u)
                nc.scalar.copy(x0_blocks[:, :, :].rearrange("p k (d b) -> p k d b", d=D),
                               x0_unit[e][:, :].rearrange("p (d k b) -> p k d b", d=D, k=2))\
                    .then_inc(blocks_ready, 1)

            def copy_x1(u, t, e):
                act.wait_ge(z_used, NI if isinstance(u, int) and u == 0 else made(u - 1, ("x1", NI - 1)))
                if not (isinstance(u, int) and u < 1):
                    for j in range(NJ):
                        act.wait_ge(B_in[1 - e][j], 32 * (t + e))
                after(act, z1_ready, u)
                nc.scalar.copy(x1_sb[:, :], ps_x1[:, :]).then_inc(x1_copied, 1)

            def copy_x2(u, e, products):
                act.wait_ge(z_used, products)
                after(act, x2_turned, u)
                nc.scalar.copy(x2_sb[:, :].rearrange("p (k d b) -> p k d b", d=D, b=RB),
                               ps_x2[e][:, :].rearrange("p (d k b) -> p k d b", d=D, b=RB)).then_inc(x2_copied, 1)

            def copy_x2_rows(u):
                act.wait_ge(x2_turned, u + 1)
                after(act, g_summed, 2 * u)
                nc.scalar.copy(x2_rows[:, :, :].rearrange("p k n -> p (k n)"), ps_x2r[:, :])\
                    .then_inc(x2r_copied, 1)

            def spread_x0(u, e):
                act.wait_ge(x0r_turned, u + 1)
                after(act, g_summed, 2 * (u - 1))
                for b in range(RB):
                    last = nc.scalar.activation(
                        x0_diag[e][:, :, :, 0:F // 2, b].rearrange("p k a j -> p k j a"),
                        ps_x0r[:, 0:256].rearrange("p (k f) -> p k f", f=32)[:, :, 0:F]
                        .rearrange("p k (j a) -> p k j a", a=2),
                        ACT.Copy, scale=mask_sb[:, b:b + 1])
                last.then_inc(diag_ready, 1)

            def copy_g(u, g, w, q):
                act.wait_ge(g_summed, 2 * u + q + 1)
                if w == 0 and q == 0:
                    after(act, z3_summed, g)
                    after(act, z12_ready, 4 * g)
                at = GQ * q + ROWS_Q * w
                nc.scalar.copy(
                    G[:, :, at:at + ROWS_Q].rearrange("p j (k b) -> p k j b", b=RB),
                    ps_g[q][:, 0:KB * J3 * RB].rearrange("p (k j b) -> p k j b", k=KB, j=J3))\
                    .then_inc(g_copied, 1)

            def copy_z12(g):
                act.wait_ge(z1_ready, W * (g + 1))
                act.wait_ge(g_copied, 2 * W * (g + 1))
                after(act, h1_summed, M1 // 128 * g)
                for q in range(2):
                    nc.scalar.copy(z1_dense[0:H, GQ * q:GQ * (q + 1)],
                                   z1_q[H * q:H * (q + 1), bass.ds(GQ * g, GQ)]).then_inc(z12_ready, 1)
                nc.scalar.copy(z1_dense[H:H + DENSE, :], dense_sb[:, bass.ds(GROWS * g, GROWS)])\
                    .then_inc(z12_ready, 1)
                nc.scalar.copy(z23[0:H, :], G[0:H, J3 - 1, :]).then_inc(z12_ready, 1)

            def copy_z3(g):
                act.wait_ge(z3_summed, g + 1)
                for q in range(2):
                    nc.scalar.copy(z23[H:2 * H, GQ * q:GQ * (q + 1)], ps_tower[H * (1 - q):H * (2 - q), 0:GQ])\
                        .then_inc(z3_ready, 1)

            def relu_h1(g, m, banks=(ps_tower,)):
                act.wait_ge(h1_summed, M1 // 128 * g + m + 1)
                if m == 0:
                    after(act, h2_summed, M2 // 128 * g)
                nc.scalar.activation(h1[m][:, :], banks[m % len(banks)][:, 0:GROWS], ACT.Relu, bias=bt1_sb[:, m:m + 1])\
                    .then_inc(h1_ready, 1)

            def relu_h2(g, m, banks=(ps_tower,)):
                act.wait_ge(h2_summed, M2 // 128 * g + m + 1)
                if m == 0:
                    after(act, y_summed, g)
                nc.scalar.activation(h2[m][:, :], banks[m % len(banks)][:, 0:GROWS], ACT.Relu, bias=bt2_sb[:, m:m + 1])\
                    .then_inc(h2_ready, 1)

            def copy_y(g):
                act.wait_ge(y_summed, g + 1)
                nc.scalar.copy(y_sb[:, bass.ds(GROWS * g, GROWS)], ps_tower[0:1, 0:GROWS]).then_inc(y_ready, 1)

            def slot(g, w, back=True, front=False, towers=True, ahead=2):
                t, e = 2 * g + w // 2, w % 2
                u = W * g + w
                if back:
                    copy_x2(u - 1, 1 - e, made(u - 1, ("x2", NP2 - 1)))
                    copy_x2_rows(u - 1)
                order_x0(u, t, e)
                if ahead > 0:
                    copy_x1(u + 1, t + e, 1 - e)
                if towers and w == 1:
                    relu_h1(g - 1, 0)
                if towers and w == 2:
                    relu_h1(g - 1, 3)
                if towers and w == 3:
                    relu_h2(g - 1, 1)
                spread_x0(u, e)
                if back:
                    before = (g - 1, W - 1) if w == 0 else (g, w - 1)
                    copy_g(u - 1, *before, 0)
                    copy_g(u - 1, *before, 1)
                if towers and w == 0:
                    copy_z12(g - 1)
                if towers and w == 1:
                    relu_h1(g - 1, 1)
                if e == 1 and front:
                    copy_x0(t + 2)
                    store_x0(t + 2)
                if ahead > 1:
                    complete_a(t + 1, e)
                if towers and w == 0:
                    copy_z3(g - 1)
                if towers and w == 1:
                    relu_h1(g - 1, 2)
                if towers and w == 2:
                    relu_h2(g - 1, 0)
                if towers and w == 3:
                    copy_y(g - 1)

            def copy_small(k):
                act.wait_ge(hot_used, sum(chunks[:k + 1]))
                for g in range(4):
                    for half in range(2):
                        nc.scalar.copy(x0_small[k][g][:, half, :],
                                       ps_small[k][half][32 * g:32 * g + D, 0:TILE_ROWS]).then_inc(small_copied, 1)
                store_small(act, k, 0, part_stored[k + 1], range(4) if k == 0 else (0, 1))

            copy_small(0)
            act.wait_ge(x0_turned, 1)
            nc.scalar.copy(x0_cols[:, 0, :], ps_x0[:, 0:TILE_ROWS]).then_inc(x0_copied, 1)
            act.wait_ge(x0_copied, 1)
            store_x0_part(0, 0, part_stored[0])
            store_x0_part(0, NI, part_stored[0])
            copy_small(1)
            complete_a(0, 0)
            copy_x1(0, 0, 0)
            complete_a(0, 1)
            copy_x0(1)
            store_x0(1)
            act.wait_ge(mask_in, 16)
            for w in range(W):
                slot(0, w, back=w > 0, front=w in (1, 3), towers=False)
            act.wait_ge(tower_in, 16 * 8)
            with act.Fori(1, GROUPS - 1) as g:
                for w in range(W):
                    slot(g, w, front=w in (1, 3))
            for w in range(W):
                slot(GROUPS - 1, w, ahead=min(2, W - 1 - w))
            copy_x2(UNITS - 1, 1, PER_SLOT * UNITS)
            copy_x2_rows(UNITS - 1)
            for q in range(2):
                copy_g(UNITS - 1, GROUPS - 1, W - 1, q)
            copy_z12(GROUPS - 1)
            copy_z3(GROUPS - 1)
            for m in range(M1 // 128):
                relu_h1(GROUPS - 1, m, (ps_tower, ps_x0))
            for m in range(M2 // 128):
                relu_h2(GROUPS - 1, m, (ps_tower, ps_x0))
            copy_y(GROUPS - 1)


def kernel(**inputs):
    import numpy as np
    import concourse.bacc as bacc
    from concourse import mybir as mb
    from concourse.bass_utils import run_bass_kernel_spmd

    a = {k: np.asarray(v) for k, v in inputs.items()}
    rows = [a[f"tbl_{f}"].shape[0] for f in range(F)]
    by_size = sorted(range(F), key=lambda f: rows[f])
    sets = [by_size[:FR], by_size[FR:SETS * FR]]
    order = by_size[SETS * FR:] + sets[0] + sets[1]
    most = [max(rows[f] for f in fs) for fs in sets]
    cr = max(-(-m // -(-m // 128)) for m in most)
    chunks = [-(-m // cr) for m in most]
    small_tables = np.zeros((FR, sum(chunks) * cr, D), np.float32)
    for k, fs in enumerate(sets):
        at = cr * sum(chunks[:k])
        for n, f in enumerate(fs):
            small_tables[n, at:at + rows[f]] = a[f"tbl_{f}"]
    ids = a["ids"][:, order]
    w0 = a["L0_rec_W0"].reshape(F, F, H)[order][:, order]
    w0a = np.zeros((HR, FR, NI, H), w0.dtype)
    w0b = np.zeros((HR, FR, NI, H), w0.dtype)
    for i in range(NI):
        for g in range(HR):
            w0a[g, :, i] = w0[FR * i:FR * (i + 1), (FR * i + g) % F]
            if g >= FR:
                w0b[g, :, i] = w0[(FR * i + g) % F, FR * i:FR * (i + 1)]
    w1 = a["L0_rec_W1"].reshape(F, H, H)[order].reshape(NI, FR, NJ, HR, H).transpose(3, 1, 0, 2, 4)
    w2 = a["L0_rec_W2"].reshape(F, H, H)[order].reshape(F // 2, 128, H).transpose(1, 0, 2)
    wt1 = a["W_top1"]
    arrays = {
        "dense_t": a["dense_ctx"].reshape(GROUPS, W, 2, ROWS_Q, DENSE).transpose(4, 0, 2, 1, 3).reshape(DENSE, BATCH),
        "ids": ids.reshape(TILES, 128, F).transpose(1, 0, 2).reshape(128, TILES * F),
        "small_ids": ids[0:TILE_ROWS, FR:].transpose(1, 0).reshape(SETS, FR * TILE_ROWS),
        "small_tables": small_tables.reshape(FR, sum(chunks), cr, D).transpose(2, 1, 0, 3),
        "small_rows": np.arange(max(chunks) * cr, dtype=np.float32).reshape(max(chunks), cr).transpose(1, 0),
        "w0a": w0a.reshape(128, NI, H),
        "w0b": w0b.reshape(128, NI, H),
        "w1": w1.reshape(128, NP2, H),
        "w2": w2,
        "wt1_z1_dense": np.concatenate([wt1[0:H], wt1[3 * H:]], axis=0),
        "wt1_z2_z3": wt1[H:3 * H],
        "bt1": a["b_top1"].reshape(M1 // 128, 128).transpose(1, 0),
        "wt2": a["W_top2"].reshape(M1 // 128, 128, M2).transpose(1, 0, 2),
        "bt2": a["b_top2"].reshape(M2 // 128, 128).transpose(1, 0),
        "wt3": a["W_top3"].reshape(M2 // 128, 128).transpose(1, 0),
        "ident": np.eye(128, dtype=np.float32),
        "mask": np.tile(np.eye(RB, dtype=np.float32), (128 // RB, 1)),
    }
    for f in range(F):
        arrays[f"tbl_{f}"] = a[f"tbl_{f}"]
    nc = bacc.Bacc("TRN2", target_bir_lowering=False, num_devices=1)
    arrays = {k: np.ascontiguousarray(v) for k, v in arrays.items()}
    ap = {k: nc.dram_tensor(k, v.shape, mb.dt.from_np(v.dtype), kind="ExternalInput").ap()
          for k, v in arrays.items()}
    out = nc.dram_tensor("y", (1, BATCH), F32, kind="ExternalOutput").ap()
    cin_tower(nc, ap["dense_t"], ap["ids"], [ap[f"tbl_{f}"] for f in order],
              ap["small_ids"], ap["small_tables"], ap["small_rows"], chunks, ap["w0a"], ap["w0b"],
              ap["w1"], ap["w2"], (ap["wt1_z1_dense"], ap["wt1_z2_z3"]), ap["bt1"], ap["wt2"], ap["bt2"],
              ap["wt3"], ap["ident"], ap["mask"], out)
    y = run_bass_kernel_spmd(nc, [arrays], core_ids=[0]).results[0]["y"]
    return y.reshape(GROUPS, 2, W, ROWS_Q).transpose(0, 2, 1, 3).reshape(BATCH, 1)
```
